# Optimizing a Trainium2 kernel written in Bass

```python
import numpy as np
import jax
import jax.numpy as jnp

def _softmax(x, axis=-1):
    return jax.nn.softmax(x, axis=axis)

def _gelu(x):
    return jax.nn.gelu(x, approximate=True)

def _silu(x):
    return jax.nn.silu(x)

def _sigmoid(x):
    return jax.nn.sigmoid(x)

def _layernorm(x, axis=-1, eps=1e-05):
    m = jnp.mean(x, axis=axis, keepdims=True)
    v = jnp.var(x, axis=axis, keepdims=True)
    return (x - m) / jnp.sqrt(v + eps)

def _scatter_add(tgt, idx, src, axis=0):
    return tgt.at[idx].add(src)

def _segment_sum(src, seg, n):
    return jax.ops.segment_sum(src, seg, n)
kernel_name = 'mk_xattn_ffn_d1_seqx_r8_216fbb'

def setup_inputs(seed: int=0):
    np.random.seed(seed)
    _w = jnp.asarray

    def _rec_inputs():
        import jax
        import jax.numpy as jnp
        _rk = jax.random.key(seed)
        x = 7.22e-05 + 1 * jax.random.normal(jax.random.fold_in(_rk, 1), (32, 64, 256), jnp.float32)
        _lenS = 64 - jax.random.randint(jax.random.fold_in(_rk, 7), (32,), 0, max(1, 64 // 4) + 1, jnp.int32)
        _lenS2 = 64 - jax.random.randint(jax.random.fold_in(_rk, 8), (32,), 0, max(1, 64 // 4) + 1, jnp.int32)
        _ctx_2048P = jax.random.normal(jax.random.fold_in(_rk, 11), (32, 16, 256), jnp.float32)
        _ctx_2048c = jax.random.dirichlet(jax.random.fold_in(_rk, 511), 0.3 * jnp.ones((16,), jnp.float32), (32, 64))
        _ctx_2048t = jnp.einsum('bsk,bkd->bsd', _ctx_2048c, _ctx_2048P)
        _ctx_2048t = _ctx_2048t * jax.lax.rsqrt(jnp.mean(jnp.square(_ctx_2048t)) + 1e-12) * 0.953939
        ctx_2048 = 4.13588e-05 + 0.999923 * (_ctx_2048t + 0.3 * jax.random.normal(jax.random.fold_in(_rk, 611), (32, 64, 256), jnp.float32))
        return (x, ctx_2048)
    x, ctx_2048 = _rec_inputs()

    def _L0_xattn_setup():
        import jax, jax.numpy as jnp
        import numpy as np
        BS, S, DK = (8, 64, 256)
        key = jax.random.key(seed)
        kq, kk, kv = jax.random.split(key, 3)
        q = jax.random.normal(kq, (BS, S, DK), dtype=jnp.float32)
        k = jax.random.normal(kk, (BS, S, DK), dtype=jnp.float32)
        v = jax.random.normal(kv, (BS, S, DK), dtype=jnp.float32)
        return {'q': q, 'k': k, 'v': v}
    _L0_xattn_all = _L0_xattn_setup()
    _L0_xattn_in = {k: v for k, v in _L0_xattn_all.items() if k in ()}
    del _L0_xattn_all

    def _L0_ffn_setup():
        import jax, jax.numpy as jnp
        import numpy as np
        TOPK = 2
        N_EXPERTS = 8
        ROUTE_SCALE = 1.0
        key = jax.random.key(seed)
        ks = jax.random.split(key, 7)
        B, T, C = (4, 256, 256)
        H = 176
        HS = 352
        E = N_EXPERTS
        s = 0.02
        return {'x': jax.random.normal(ks[0], (B, T, C), jnp.float32), 'gate_w': jax.random.normal(ks[1], (E, C), jnp.float32) * s, 'gate_bias': jnp.zeros((E,), jnp.float32), 'shared_gw': jax.random.normal(ks[2], (2 * HS, C), jnp.float32) * s, 'shared_dw': jax.random.normal(ks[3], (C, HS), jnp.float32) * s, 'up_w': jax.random.normal(ks[4], (E, 2 * H, C), jnp.float32) * s, 'down_w': jax.random.normal(ks[5], (E, C, H), jnp.float32) * s}
    _L0_ffn_all = _L0_ffn_setup()
    _L0_ffn_in = {k: v for k, v in _L0_ffn_all.items() if k in ('gate_w', 'gate_bias', 'shared_gw', 'shared_dw', 'up_w', 'down_w')}
    del _L0_ffn_all
    return {'x': x, 'ctx_2048': ctx_2048, 'L0_ffn_gate_w': _L0_ffn_in['gate_w'], 'L0_ffn_gate_bias': _L0_ffn_in['gate_bias'], 'L0_ffn_shared_gw': _L0_ffn_in['shared_gw'], 'L0_ffn_shared_dw': _L0_ffn_in['shared_dw'], 'L0_ffn_up_w': _L0_ffn_in['up_w'], 'L0_ffn_down_w': _L0_ffn_in['down_w']}

def reference(x, ctx_2048, L0_ffn_gate_w, L0_ffn_gate_bias, L0_ffn_shared_gw, L0_ffn_shared_dw, L0_ffn_up_w, L0_ffn_down_w):
    import jax
    import jax.numpy as jnp

    def _L0_xattn_ref(q, k, v):
        import jax, jax.numpy as jnp
        import numpy as np
        BS, S, DK = (8, 64, 256)
        dk = q.shape[-1]
        scale = 1.0 / jnp.sqrt(jnp.asarray(dk, dtype=q.dtype))
        scaled = jnp.einsum('bsd,bse->bde', q, k) * scale
        attn = jax.nn.softmax(scaled, axis=1)
        out = jnp.einsum('bde,bse->bsd', attn, v)
        return out

    def _L0_ffn_ref(x, gate_w, gate_bias, shared_gw, shared_dw, up_w, down_w):
        import jax, jax.numpy as jnp
        import numpy as np
        TOPK = 2
        N_EXPERTS = 8
        ROUTE_SCALE = 1.0
        B, T, C = x.shape
        xf = x.reshape(-1, C)
        yg = xf @ shared_gw.T
        y, g = jnp.split(yg, 2, axis=-1)
        shared = jax.nn.silu(g) * y @ shared_dw.T
        scores = jax.nn.sigmoid(xf @ gate_w.T)
        _, topk_idx = jax.lax.top_k(scores + gate_bias, TOPK)
        w = jnp.take_along_axis(scores, topk_idx, axis=-1)
        w = w / jnp.sum(w, axis=-1, keepdims=True) * ROUTE_SCALE
        out = jnp.zeros_like(xf)
        for e in range(N_EXPERTS):
            we = jnp.sum(jnp.where(topk_idx == e, w, 0.0), axis=-1)
            gu = xf @ up_w[e].T
            g_e, u_e = jnp.split(gu, 2, axis=-1)
            h = jax.nn.silu(g_e) * u_e
            out = out + h @ down_w[e].T * we[:, None]
        return (shared + out).reshape(B, T, C)
    x = x + _L0_xattn_ref(_layernorm(x, axis=-1), ctx_2048, ctx_2048)
    x = x + _L0_ffn_ref(_layernorm(x, axis=-1), L0_ffn_gate_w, L0_ffn_gate_bias, L0_ffn_shared_gw, L0_ffn_shared_dw, L0_ffn_up_w, L0_ffn_down_w)
    return x

_drawn_inputs = setup_inputs


def setup_inputs(seed=0):
    import zlib

    import numpy as np

    out = dict(_drawn_inputs(seed))
    spreads = {'L0_ffn_gate_bias': (0.0, 0.8)}
    factors = {'L0_ffn_gate_w': 8.0,
     'L0_ffn_shared_gw': 3.067,
     'L0_ffn_shared_dw': 3.078,
     'L0_ffn_up_w': 6.143,
     'L0_ffn_down_w': 6.16}
    for name, (base, spread) in spreads.items():
        noise = np.random.default_rng([zlib.crc32(name.encode()), seed]).standard_normal(out[name].shape)
        drawn = base * np.exp(spread * noise) if base else spread * noise
        out[name] = jnp.asarray(drawn.astype(out[name].dtype))
    for name, factor in factors.items():
        out[name] = (out[name] * factor).astype(out[name].dtype)
    return out
```

```python
import concourse.bass as bass
from concourse import mybir
from contextlib import ExitStack


def xattn_moe_kernel(nc, x, ctx_kv, up_wT, down_wT, shared_upT, shared_dnT, gate_wT, gate_bias, out):
    F32, F32R, BF16 = mybir.dt.float32, mybir.dt.float32r, mybir.dt.bfloat16
    U32, I32 = mybir.dt.uint32, mybir.dt.int32
    ALU, ACT, AX = mybir.AluOpType, mybir.ActivationFunctionType, mybir.AxisListType

    P = 128
    TOK, D = x.shape
    S = 64
    B2 = P // S
    NT = TOK // P
    DC = D // P
    E = up_wT.shape[1]
    K = 2
    H = up_wT.shape[2] // (2 * DC)
    HS = shared_upT.shape[2] // 2
    SC = -(-HS // P)
    CHUNK = [min(P, HS - c * P) for c in range(SC)]
    SLOTS = (K * TOK + E * (P - 1)) // P
    ROW = D + 2
    TRASH = K * TOK
    SCALE = float(D) ** -0.5
    EPS = 1e-5
    GT = 2
    GN = GT * P
    NG = NT // GT
    RB = 4
    NL = 4

    slot_rows = nc.dram_tensor("slot_rows", [SLOTS * P, ROW], F32, kind="Internal").ap()
    expert_out = nc.dram_tensor("expert_out", [TRASH + SLOTS * P, D], F32, kind="Internal").ap()

    with ExitStack() as stack:
        def sb(name, shape, dt=F32):
            return stack.enter_context(nc.sbuf_tensor(name, shape, dt))

        def sem(name):
            return stack.enter_context(nc.semaphore(name))

        bank = [stack.enter_context(nc.psum_tensor(f"bank{i}", [P, 512], F32)) for i in range(8)]

        x_all = sb("x_all", [P, NT, D])
        z_all = sb("z_all", [P, NT, ROW])
        zTh = sb("zTh", [P, DC, TOK], F32R)
        zTl = sb("zTl", [P, DC, TOK], F32R)
        uph = sb("uph", [P, E, DC * 2 * H], F32R)
        upl = sb("upl", [P, E, DC * 2 * H], F32R)
        dnh = sb("dnh", [P, E, DC * D], F32R)
        dnl = sb("dnl", [P, E, DC * D], F32R)
        suh = sb("suh", [P, DC, 2 * HS], F32R)
        sul = sb("sul", [P, DC, 2 * HS], F32R)
        sdh = sb("sdh", [P, SC, D], F32R)
        sdl = sb("sdl", [P, SC, D], F32R)
        gws = sb("gws", [P, DC * E])
        gwh = sb("gwh", [P, DC * E], F32R)
        gwl = sb("gwl", [P, DC * E], F32R)
        bias = sb("bias", [P, E])
        cr = sb("cr", [P, NL, D])
        q = sb("q", [P, 2, D])
        kh = sb("kh", [P, 2, D], F32R)
        kl = sb("kl", [P, 2, D], F32R)
        qh = sb("qh", [P, 2, D], F32R)
        ql = sb("ql", [P, 2, D], F32R)
        att = sb("att", [P, 2, B2 * DC * D])
        vT = sb("vT", [P, 2, DC, B2, S])
        stats = sb("stats", [P, 2, 6])
        mv = sb("mv", [P, 2, 2])
        rstd = sb("rstd", [P, 2, 1])
        stats2 = sb("stats2", [P, 2, 6])
        mv2 = sb("mv2", [P, 2, 2])
        rstd2 = sb("rstd2", [P, 2, 1])
        mx = sb("mx", [P, 2, DC * B2])
        nb = sb("nb", [P, 2, DC * B2])
        rs = sb("rs", [P, 2, DC * B2])
        ri = sb("ri", [P, 2, DC * B2])
        ident = sb("ident", [P, P])
        below = sb("below", [P, P], BF16)
        ones = sb("ones", [P, P], BF16)
        mhalf = sb("mhalf", [P, 1])
        iota_e = sb("iota_e", [P, E])
        lower = sb("lower", [P, E, E])
        iota_n = sb("iota_n", [P, NT])
        slotno = sb("slotno", [P, SLOTS])
        tileno = sb("tileno", [1, SLOTS])
        no_token = sb("no_token", [P, D])
        no_place = sb("no_place", [P, SLOTS, 2])
        el = sb("el", [P, NT, E])
        sg = sb("sg", [P, NT, E])
        sbias = sb("sbias", [P, NT, E])
        top = sb("top", [P, NT, E])
        tidx = sb("tidx", [P, NT, E], U32)
        fidx = sb("fidx", [P, NT, K])
        pick = sb("pick", [P, K, NT, E])
        both = sb("both", [P, NT, E], BF16)
        wk = sb("wk", [P, K, NT])
        wsum = sb("wsum", [P, 2, NT])
        big = sb("big", [P, E, NT])
        small = sb("small", [P, 4, E])
        tri = sb("tri", [P, E, E])
        dest = sb("dest", [P, K, NT])
        desti = sb("desti", [P, K, NT], U32)
        cmp_t = sb("cmp_t", [1, SLOTS, E])
        tab_f = sb("tab_f", [1, SLOTS])
        tab = sb("tab", [1, SLOTS], I32)
        s_sg = sb("s_sg", [P, 2, GN])
        s_hm = sb("s_hm", [P, 2, GN])
        s_hh = sb("s_hh", [P, 2, SC, GN], F32R)
        s_hl = sb("s_hl", [P, 2, SC, GN], F32R)
        yi = sb("yi", [P, SLOTS], U32)

        z_flat = z_all[:, :, :].rearrange("p t c -> p (t c)")
        SU, SD = DC * 2 * HS, SC * D
        SRAW = NT * ROW - SU - SD
        su_raw = z_flat[:, SRAW:SRAW + SU]
        sd_raw = z_flat[:, SRAW + SU:SRAW + SU + SD]
        FIRST_RAW = SRAW // ROW
        att_flat = att[:, :, :].rearrange("p j c -> p (j c)")
        xs = [att_flat[:, i * ROW:(i + 1) * ROW] for i in range(3)]
        ys = [att_flat[:, 3 * ROW + i * D:3 * ROW + (i + 1) * D] for i in range(3)]
        esg = [att_flat[:, 3 * (ROW + D) + i * H:3 * (ROW + D) + (i + 1) * H] for i in range(2)]
        xh, xl, hh, hl, hm = kh, kl, qh, ql, q

        ps_s = [[bank[0], bank[1]], [bank[2], bank[3]]]
        ps_c, ps_o = bank[4][:, 0:D], bank[5][:, 0:D]
        zT, logits = bank[6][:, 0:D], bank[6][:, D:D + E]
        rank = bank[7][:, 0:(NT + 1) * E]
        s_gu = [bank[0], bank[1], bank[2]]
        s_dn = [bank[3][:, 0:D], bank[4][:, 0:D]]
        e_xt = bank[6][:, 0:D]
        e_gu = [bank[0], bank[1]]
        e_ht = bank[5][:, 0:D]
        e_y = [bank[7][:, 0:D], bank[2][:, 0:D]]

        x_in = [sem(f"x_in{i}") for i in range(NL)]
        c_in = [sem(f"c_in{i}") for i in range(NL)]
        g_in, sw_in, pads_in = sem("g_in"), sem("sw_in"), sem("pads_in")
        ew_in = [sem("ew_in0"), sem("ew_in1")]
        const_done = sem("const_done")
        id_done = sem("id_done")
        pad_row = sem("pad_row")
        ztail_done = sem("ztail_done")
        var_done, rstd_done, q_done = sem("var_done"), sem("rstd_done"), sem("q_done")
        kq_high, kq_low = sem("kq_high"), sem("kq_low")
        sc_done, ct_done, nb_done, exp_done = sem("sc_done"), sem("ct_done"), sem("nb_done"), sem("exp_done")
        vt_done, out_done, x1_done = sem("vt_done"), sem("out_done"), sem("x1_done")
        var2_done, rstd2_done, z_done = sem("var2_done"), sem("rstd2_done"), sem("z_done")
        zt_done, zh_done, zl_done = sem("zt_done"), sem("zh_done"), sem("zl_done")
        lg_done, el_done = sem("lg_done"), sem("el_done")
        gw_done, sw_high, sw_low = sem("gw_done"), sem("sw_high"), sem("sw_low")
        ew_high, ew_low = sem("ew_high"), sem("ew_low")
        both_done, rank_done = sem("both_done"), sem("rank_done")
        rank_read = sem("rank_read")
        dest_done, tab_done, sent = sem("dest_done"), sem("tab_done"), sem("sent")
        sup_done, ssg_done, shm_done = sem("sup_done"), sem("ssg_done"), sem("shm_done")
        shh_done, shl_done, sdn_done, sacc_done = sem("shh_done"), sem("shl_done"), sem("sdn_done"), sem("sacc_done")
        xs_in = [sem(f"xs_in{i}") for i in range(3)]
        yi_done = sem("yi_done")
        ext_done, exh_done, exl_done = sem("ext_done"), sem("exh_done"), sem("exl_done")
        eup_done, esg_done, ehm_done = sem("eup_done"), sem("esg_done"), sem("ehm_done")
        eht_done, ehh_done, ehl_done = sem("eht_done"), sem("ehh_done"), sem("ehl_done")
        edn_done, ey_done = sem("edn_done"), sem("ey_done")
        y_out = [sem(f"y_out{i}") for i in range(3)]
        yk_in = [sem(f"yk_in{i}") for i in range(4)]
        fin_done, hm_pad = sem("fin_done"), sem("hm_pad")
        stored = sem("stored")
        c_dve = sem("c_dve")
        c_pool = sem("c_pool")

        block = stack.enter_context(nc.Block())

        STEPS = range(-2, NT + 4)

        def live(t):
            return 0 <= t < NT

        NPC = NG * SC
        PIECES = range(NPC + SC)

        def pieces_in(p):
            return range((p - NT) * PER_STEP, (p - NT + 1) * PER_STEP) if p >= NT else []

        PER_STEP = 1
        REST = range(4 * PER_STEP, len(PIECES))

        pieces = [(uph[:, e, :], upl[:, e, :], up_wT[:, e, :]) for e in range(E)] + \
                 [(dnh[:, e, :], dnl[:, e, :], down_wT[:, e, :]) for e in range(E)]
        order = [n for e in range(E) for n in (e, E + e)]
        pieces = [pieces[n] for n in order]
        NP = len(pieces)

        def stage(n):
            return att[:, n % 2, 0:pieces[n][2].shape[1]]

        ESTEPS = range(SLOTS + 3)

        def slot(t):
            return 0 <= t < SLOTS

        @block.sync
        def _(sp):
            xv = x.rearrange("(t p) d -> t p d", p=P)
            cv = ctx_kv.rearrange("(t p) d -> t p d", p=P)

            def load(p):
                j = p % NL
                if p >= NL:
                    sp.wait_ge(x_in[j], 16 * (p // NL))
                sp.dma_start(x_all[:, p, :], xv[p]).then_inc(x_in[j], 16)
                if p >= NL:
                    sp.wait_ge(kq_low, p - NL + 1)
                    sp.wait_ge(ct_done, p - NL + 1)
                sp.dma_start(cr[:, j, :], cv[p]).then_inc(c_in[j], 16)

            load(0)
            load(1)
            sp.dma_start(gws[:], gate_wT).then_inc(g_in, 16)
            sp.dma_start(bias[:], gate_bias).then_inc(g_in, 16)
            sp.dma_start(su_raw, shared_upT.rearrange("p c f -> p (c f)")).then_inc(sw_in, 16)
            sp.dma_start(sd_raw, shared_dnT.rearrange("p c f -> p (c f)")).then_inc(sw_in, 16)
            load(2)
            load(3)
            sp.wait_ge(pad_row, 3)
            rows = slot_rows.rearrange("(t p) c -> p t c", p=P)
            sp.dma_start(rows[:, :, 0:D], no_token[:, :].unsqueeze(1).broadcast_to([P, SLOTS, D])).then_inc(pads_in, 16)
            sp.dma_start(rows[:, :, D:ROW], no_place[:, :, :]).then_inc(pads_in, 16)
            for p in range(4, NT):
                load(p)
            sp.wait_ge(out_done, NT)
            for n in range(NP):
                if n >= 2:
                    sp.wait_ge(ew_low, n - 1)
                sp.dma_start(stage(n), pieces[n][2]).then_inc(ew_in[n % 2], 16)
            sp.wait_ge(ew_low, NP)
            sp.wait_ge(sent, 16 * K * NT)
            sv = slot_rows.rearrange("(t p) c -> t p c", p=P)
            for t in range(SLOTS):
                if t >= 3:
                    sp.wait_ge(ext_done, t - 2)
                    sp.wait_ge(yi_done, t - 2)
                sp.dma_start(xs[t % 3], sv[t]).then_inc(xs_in[t % 3], 16)
            for i in range(3):
                sp.wait_ge(y_out[i], 16 * len(range(i, SLOTS, 3)))
            yv = expert_out[0:TRASH, :].rearrange("(t p k) d -> t p (k d)", p=P, k=K)
            for t in range(NT):
                if t >= 4:
                    sp.wait_ge(fin_done, t - 3)
                sp.dma_start(att_flat[:, (t % 4) * K * D:(t % 4 + 1) * K * D], yv[t]).then_inc(yk_in[t % 4], 16)
            sp.wait_ge(stored, 16 * NT)

        @block.gpsimd
        def _(pool):
            def iota(ap, pattern, base, mult):
                return nc.gpsimd.iota(ap, pattern, base=base, channel_multiplier=mult,
                                      allow_small_or_imprecise_dtypes=True)

            nc.gpsimd.memset(mhalf[:], -0.5)
            nc.gpsimd.memset(ident[:], 0.0).then_inc(c_pool, 1)
            pool.wait_ge(c_pool, 1)
            nc.gpsimd.affine_select(out=ident[:], in_=ident[:], compare_op=ALU.not_equal, fill=1.0,
                                    base=0, pattern=[[-1, P]], channel_multiplier=1).then_inc(id_done, 1)
            n_pool = [1]

            def prepare():
                nc.gpsimd.memset(no_token[:], 0.0).then_inc(pad_row, 1)
                iota(no_place[:, :, 0], [[P, SLOTS]], TRASH, 1).then_inc(pad_row, 1)
                nc.gpsimd.memset(no_place[:, :, 1], -1.0).then_inc(pad_row, 1)
                iota(iota_e[:], [[1, E]], 0, 0).then_inc(const_done, 1)
                iota(iota_n[:], [[P, NT]], 0, 0).then_inc(const_done, 1)
                iota(slotno[:], [[P, SLOTS]], 0, 1).then_inc(const_done, 1)
                iota(tileno[:], [[1, SLOTS]], 0, 0).then_inc(const_done, 1)
                nc.gpsimd.memset(ones[:], 1.0).then_inc(const_done, 1)
                nc.gpsimd.memset(below[:], 1.0).then_inc(c_pool, 1)
                nc.gpsimd.memset(lower[:], 1.0).then_inc(c_pool, 1)
                n_pool[0] += 2
                pool.wait_ge(c_pool, n_pool[0])
                nc.gpsimd.affine_select(out=below[:], in_=below[:], compare_op=ALU.is_gt, fill=0.0,
                                        base=0, pattern=[[1, P]], channel_multiplier=-1).then_inc(const_done, 1)
                nc.gpsimd.affine_select(out=lower[:], in_=lower[:], compare_op=ALU.is_gt, fill=0.0,
                                        base=0, pattern=[[1, E], [-1, E]], channel_multiplier=0).then_inc(const_done, 1)

            def gate_split():
                pool.wait_ge(g_in, 32)
                nc.gpsimd.tensor_copy(gwh[:], gws[:]).then_inc(c_pool, 1)
                n_pool[0] += 1
                pool.wait_ge(c_pool, n_pool[0])
                nc.gpsimd.tensor_tensor(gwl[:], gws[:], gwh[:].bitcast(F32), ALU.subtract).then_inc(gw_done, 1)

            def shared_low(piece):
                pool.wait_ge(sw_high, piece + 1)
                if piece < DC:
                    r = slice(piece * 2 * HS, (piece + 1) * 2 * HS)
                    nc.gpsimd.tensor_tensor(sul[:, piece, :], su_raw[:, r], suh[:, piece, :].bitcast(F32),
                                            ALU.subtract).then_inc(sw_low, 1)
                else:
                    nc.gpsimd.tensor_tensor(sdl[:, :, :].rearrange("p c d -> p (c d)"), sd_raw,
                                            sdh[:, :, :].rearrange("p c d -> p (c d)").bitcast(F32),
                                            ALU.subtract).then_inc(sw_low, 1)

            prepare()
            gate_split()
            for p in STEPS:
                if live(p - 2):
                    k, j = p - 2, p % 2
                    pool.wait_ge(var2_done, k + 1)
                    nc.gpsimd.tensor_tensor(rstd2[:, j, :], mv2[:, j, 1:2], mhalf[:], ALU.pow).then_inc(rstd2_done, 1)
                if live(p + 1):
                    k, j = p + 1, (p + 1) % 2
                    if k >= 2:
                        pool.wait_ge(sc_done, B2 * (k - 1))
                    pool.wait_ge(kq_high, 2 * k + 1)
                    nc.gpsimd.tensor_tensor(kl[:, j, :], cr[:, k % NL, :], kh[:, j, :].bitcast(F32), ALU.subtract)
                    pool.wait_ge(kq_high, 2 * k + 2)
                    nc.gpsimd.tensor_tensor(ql[:, j, :], q[:, j, :], qh[:, j, :].bitcast(F32),
                                            ALU.subtract).then_inc(kq_low, 1)
                if live(p + 2):
                    k, j = p + 2, p % 2
                    pool.wait_ge(var_done, k + 1)
                    nc.gpsimd.tensor_tensor(rstd[:, j, :], mv[:, j, 1:2], mhalf[:], ALU.pow).then_inc(rstd_done, 1)
                if 1 <= p < DC + 2:
                    shared_low(p - 1)
                if p == DC + 2:
                    pool.wait_ge(sw_low, DC + 1)
                    iota(z_all[:, :, D], [[2 * P, NT]], 0, 2).then_inc(ztail_done, 1)

            pool.wait_ge(dest_done, 2)
            pool.wait_ge(ztail_done, 1)
            pool.wait_ge(z_done, NT)
            pool.wait_ge(pads_in, 32)
            for k in range(K):
                for t in range(NT):
                    nc.gpsimd.indirect_dma_start(
                        slot_rows, bass.IndirectOffsetOnAxis(ap=desti[:, k, t:t + 1], axis=0),
                        z_all[:, t, :], None).then_inc(sent, 16)
            for t in range(SLOTS):
                pool.wait_ge(ey_done, t + 1)
                pool.wait_ge(yi_done, t + 1)
                nc.gpsimd.indirect_dma_start(
                    expert_out, bass.IndirectOffsetOnAxis(ap=yi[:, t:t + 1], axis=0),
                    ys[t % 3], None).then_inc(y_out[t % 3], 16)

        @block.scalar
        def _(act):
            def copy(o, i):
                return nc.scalar.activation(o, i, ACT.Copy)

            def shared_high():
                act.wait_ge(sw_in, 32)
                for c in range(DC):
                    copy(suh[:, c, :], su_raw[:, c * 2 * HS:(c + 1) * 2 * HS]).then_inc(sw_high, 1)
                copy(sdh[:, :, :].rearrange("p c d -> p (c d)"), sd_raw).then_inc(sw_high, 1)

            def shared_piece(n):
                if n < NPC:
                    m = CHUNK[n % SC]
                    act.wait_ge(sup_done, n + 1)
                    if n >= 2:
                        act.wait_ge(shm_done, n - 1)
                    nc.scalar.activation(s_sg[0:m, n % 2, :], s_gu[n % 3][0:m, 0:GN], ACT.Silu).then_inc(ssg_done, 1)
                if 0 <= n - 1 < NPC:
                    g, c = (n - 1) // SC, (n - 1) % SC
                    m = CHUNK[c]
                    if c == 0 and g >= 2:
                        act.wait_ge(sdn_done, GT * (g - 1))
                    act.wait_ge(shm_done, n)
                    copy(s_hh[0:m, g % 2, c, :], s_hm[0:m, (n - 1) % 2, :]).then_inc(shh_done, 1)

            def expert_high(n):
                act.wait_ge(ew_in[n % 2], 16 * (n // 2 + 1))
                copy(pieces[n][0], stage(n)).then_inc(ew_high, 1)

            for p in STEPS:
                if live(p + 1):
                    k, j = p + 1, (p + 1) % 2
                    act.wait_ge(c_in[k % NL], 16 * (k // NL + 1))
                    if k >= 2:
                        act.wait_ge(sc_done, B2 * (k - 1))
                    copy(kh[:, j, :], cr[:, k % NL, :]).then_inc(kq_high, 1)
                    act.wait_ge(q_done, k + 1)
                    copy(qh[:, j, :], q[:, j, :]).then_inc(kq_high, 1)
                for b in range(B2):
                    if live(p):
                        k, j = p, p % 2
                        if k >= 2:
                            act.wait_ge(out_done, k - 1)
                        act.wait_ge(nb_done, B2 * k + b + 1)
                        for c in range(DC):
                            n = c * B2 + b
                            m = (b * DC + c) * D
                            last = nc.scalar.activation(att[:, j, m:m + D], ps_s[j][b][:, c * D:(c + 1) * D],
                                                        ACT.Exp, bias=nb[:, j, n:n + 1], scale=SCALE,
                                                        accum_out=rs[:, j, n:n + 1])
                        last.then_inc(exp_done, 1)
                    if b == 0 and live(p - 3):
                        act.wait_ge(lg_done, p - 2)
                        nc.scalar.activation(el[:, p - 3, :], logits, ACT.Exp, scale=-1.0).then_inc(el_done, 1)
                if live(p - 2):
                    k = p - 2
                    act.wait_ge(zt_done, k + 1)
                    copy(zTh[:, :, k * P:(k + 1) * P], zT.rearrange("p (c t) -> p c t", c=DC)).then_inc(zh_done, 1)
                if p == 0:
                    shared_high()
                for n in pieces_in(p):
                    shared_piece(n)
            done = 0
            for i, n in enumerate(REST):
                shared_piece(n)
                upto = (i + 1) * NP // len(REST)
                for w in range(done, upto):
                    expert_high(w)
                done = upto

            for s in ESTEPS:
                if slot(s):
                    act.wait_ge(ext_done, s + 1)
                    if s >= 2:
                        act.wait_ge(eup_done, s - 1)
                    copy(xh[:, s % 2, :], e_xt).then_inc(exh_done, 1)
                if slot(s - 1):
                    t = s - 1
                    act.wait_ge(eup_done, t + 1)
                    if t >= 2:
                        act.wait_ge(ehm_done, t - 1)
                    nc.scalar.activation(esg[t % 2], e_gu[t % 2][:, 0:H], ACT.Silu).then_inc(esg_done, 1)
                if slot(s - 2):
                    t = s - 2
                    act.wait_ge(eht_done, t + 1)
                    if t >= 2:
                        act.wait_ge(edn_done, t - 1)
                    copy(hh[:, t % 2, :], e_ht).then_inc(ehh_done, 1)
                if slot(s - 3):
                    t = s - 3
                    act.wait_ge(edn_done, t + 1)
                    if t >= 3:
                        act.wait_ge(y_out[t % 3], 16 * (t // 3))
                    copy(ys[t % 3], e_y[t % 2]).then_inc(ey_done, 1)

            ov = out.rearrange("(t p) d -> t p d", p=P)
            for t in range(NT):
                act.wait_ge(fin_done, t + 1)
                act.dma_start(ov[t], x_all[:, t, :]).then_inc(stored, 16)

        @block.vector
        def _(dve):
            chain = [0]

            def mark(ins):
                ins.then_inc(c_dve, 1)
                chain[0] += 1
                return chain[0]

            def link(ins):
                dve.wait_ge(c_dve, mark(ins))

            def stats_1(k):
                j = k % 2
                dve.wait_ge(x_in[k % NL], 16 * (k // NL + 1))
                return mark(nc.vector.bn_stats(stats[:, j, :], x_all[:, k, :]))

            def aggregate(m, st, n):
                dve.wait_ge(c_dve, n)
                return mark(nc.vector.bn_aggr(m, st))

            def plus_eps(m, n, done):
                dve.wait_ge(c_dve, n)
                nc.vector.tensor_scalar(m[:, 1:2], m[:, 1:2], EPS, None, ALU.add).then_inc(done, 1)

            def norm_1(k):
                j = k % 2
                dve.wait_ge(rstd_done, k + 1)
                if k >= 2:
                    dve.wait_ge(kq_low, k - 1)
                nc.vector.tensor_scalar(q[:, j, :], x_all[:, k, :], mv[:, j, 0:1], rstd[:, j, :],
                                        ALU.subtract, ALU.mult).then_inc(q_done, 1)

            def maxima(k, b):
                j = k % 2
                if k >= 2:
                    dve.wait_ge(exp_done, B2 * (k - 1))
                m = mx[:, j, :].rearrange("p (c b) -> p b c", b=B2)
                dve.wait_ge(sc_done, B2 * k + b + 1)
                return mark(nc.vector.tensor_reduce(m[:, b, :], ps_s[j][b][:, :].rearrange("p (c d) -> p c d", c=DC),
                                                    AX.X, ALU.max))

            def negated(k, b, n):
                j = k % 2
                m = mx[:, j, :].rearrange("p (c b) -> p b c", b=B2)
                o = nb[:, j, :].rearrange("p (c b) -> p b c", b=B2)
                dve.wait_ge(c_dve, n)
                nc.vector.tensor_scalar(o[:, b, :], m[:, b, :], -SCALE, None, ALU.mult).then_inc(nb_done, 1)

            def inverse_sums(k):
                dve.wait_ge(exp_done, B2 * (k + 1))
                return mark(nc.vector.reciprocal(ri[:, k % 2, :], rs[:, k % 2, :]))

            def values(k, n):
                j = k % 2
                dve.wait_ge(c_dve, n)
                dve.wait_ge(ct_done, k + 1)
                if k >= 2:
                    dve.wait_ge(out_done, k - 1)
                nc.vector.tensor_tensor(vT[:, j, :, :, :].rearrange("p c b s -> p (c b) s"),
                                        ps_c.rearrange("p (n s) -> p n s", s=S),
                                        ri[:, j, :].unsqueeze(2).broadcast_to([P, DC * B2, S]),
                                        ALU.mult).then_inc(vt_done, 1)

            def add_attention(k):
                dve.wait_ge(out_done, k + 1)
                nc.vector.tensor_tensor(x_all[:, k, :], ps_o, x_all[:, k, :], ALU.add).then_inc(x1_done, 1)

            def stats_2(k):
                dve.wait_ge(x1_done, k + 1)
                return mark(nc.vector.bn_stats(stats2[:, k % 2, :], x_all[:, k, :]))

            def norm_2(k):
                j = k % 2
                dve.wait_ge(rstd2_done, k + 1)
                if k == FIRST_RAW:
                    dve.wait_ge(sw_low, DC + 1)
                nc.vector.tensor_scalar(z_all[:, k, 0:D], x_all[:, k, :], mv2[:, j, 0:1], rstd2[:, j, :],
                                        ALU.subtract, ALU.mult).then_inc(z_done, 1)

            def z_low(k):
                dve.wait_ge(zh_done, k + 1)
                nc.vector.tensor_tensor(zTl[:, :, k * P:(k + 1) * P], zT.rearrange("p (c t) -> p c t", c=DC),
                                        zTh[:, :, k * P:(k + 1) * P].bitcast(F32), ALU.subtract).then_inc(zl_done, 1)

            def route(r):
                t = slice(r * RB, (r + 1) * RB)
                dve.wait_ge(el_done, (r + 1) * RB)
                link(nc.vector.tensor_scalar(sg[:, t, :], el[:, t, :], 1.0, None, ALU.add))
                link(nc.vector.reciprocal(sg[:, t, :], sg[:, t, :]))
                link(nc.vector.tensor_tensor(sbias[:, t, :], sg[:, t, :],
                                             bias[:, :].unsqueeze(1).broadcast_to([P, RB, E]), ALU.add))
                for i in range(r * RB, (r + 1) * RB):
                    last = nc.vector.max(top[:, i, :], sbias[:, i, :])
                link(last)
                for i in range(r * RB, (r + 1) * RB):
                    last = nc.vector.max_index(tidx[:, i, :], top[:, i, :], sbias[:, i, :])
                link(last)
                link(nc.vector.tensor_copy(fidx[:, t, :], tidx[:, t, 0:K]))
                for k in range(K):
                    last = nc.vector.tensor_tensor(pick[:, k, t, :], iota_e[:, :].unsqueeze(1).broadcast_to([P, RB, E]),
                                                   fidx[:, t, k:k + 1].broadcast_to([P, RB, E]), ALU.is_equal)
                link(last)
                nc.vector.tensor_tensor(both[:, t, :], pick[:, 0, t, :], pick[:, 1, t, :],
                                        ALU.add).then_inc(both_done, 1)

            def destinations():
                dve.wait_ge(rank_done, 1)
                count = rank[:, NT * E:(NT + 1) * E]
                link(nc.vector.tensor_copy(small[:, 0, :], count))
                link(nc.vector.tensor_tensor(big[:, :, :], small[:, 0, :].unsqueeze(2).broadcast_to([P, E, NT]),
                                             iota_n[:, :].unsqueeze(1).broadcast_to([P, E, NT]), ALU.is_gt))
                link(nc.vector.tensor_reduce(small[:, 1, :], big[:, :, :], AX.X, ALU.add))
                link(nc.vector.tensor_tensor(tri[:, :, :], lower[:, :, :],
                                             small[:, 1, :].unsqueeze(1).broadcast_to([P, E, E]), ALU.mult))
                link(nc.vector.tensor_reduce(small[:, 2, :], tri[:, :, :], AX.X, ALU.add))
                nc.vector.tensor_tensor(small[:, 3, :], small[:, 1, :], small[:, 2, :], ALU.add)
                link(nc.vector.scalar_tensor_tensor(sbias[:, :, :], small[:, 2, :].unsqueeze(1).broadcast_to([P, NT, E]),
                                                    float(P), rank[:, 0:NT * E].rearrange("p (t e) -> p t e", e=E),
                                                    ALU.mult, ALU.add))
                for k in range(K):
                    last = nc.vector.tensor_tensor([top, el][k][:, :, :], pick[:, k, :, :], sbias[:, :, :], ALU.mult)
                link(last)
                for k in range(K):
                    last = nc.vector.tensor_reduce(dest[:, k, :], [top, el][k][:, :, :], AX.X, ALU.add)
                link(last)
                nc.vector.tensor_copy(desti[:, :, :], dest[:, :, :]).then_inc(dest_done, 1)
                dve.wait_ge(z_done, NT)
                nc.vector.tensor_copy(z_all[:, :, D + 1], dest[:, 1, :]).then_inc(dest_done, 1)

            def table_and_weights():
                link(nc.vector.tensor_tensor(cmp_t[:, :, :], tileno[:, :].unsqueeze(2).broadcast_to([1, SLOTS, E]),
                                             small[0:1, 3, :].unsqueeze(1).broadcast_to([1, SLOTS, E]), ALU.is_ge))
                link(nc.vector.tensor_reduce(tab_f[:, :], cmp_t[:, :, :], AX.X, ALU.add))
                nc.vector.tensor_scalar(tab[:, :], tab_f[:, :], float(E - 1), None, ALU.min).then_inc(tab_done, 1)
                for k in range(K):
                    last = nc.vector.tensor_tensor([top, el][k][:, :, :], pick[:, k, :, :], sg[:, :, :], ALU.mult)
                link(last)
                for k in range(K):
                    last = nc.vector.tensor_reduce(wk[:, k, :], [top, el][k][:, :, :], AX.X, ALU.add)
                link(last)
                link(nc.vector.tensor_tensor(wsum[:, 0, :], wk[:, 0, :], wk[:, 1, :], ALU.add))
                link(nc.vector.reciprocal(wsum[:, 1, :], wsum[:, 0, :]))
                for k in range(K):
                    last = nc.vector.tensor_tensor(wk[:, k, :], wk[:, k, :], wsum[:, 1, :], ALU.mult)
                link(last)

            def shared_piece(n):
                if n < NPC:
                    m = CHUNK[n % SC]
                    dve.wait_ge(ssg_done, n + 1)
                    if n >= 2:
                        dve.wait_ge(shl_done, n - 1)
                    nc.vector.tensor_tensor(s_hm[0:m, n % 2, :], s_sg[0:m, n % 2, :], s_gu[n % 3][0:m, GN:2 * GN],
                                            ALU.mult).then_inc(shm_done, 1)
                if 0 <= n - 1 < NPC:
                    g, c = (n - 1) // SC, (n - 1) % SC
                    m = CHUNK[c]
                    dve.wait_ge(shh_done, n)
                    nc.vector.tensor_tensor(s_hl[0:m, g % 2, c, :], s_hm[0:m, (n - 1) % 2, :],
                                            s_hh[0:m, g % 2, c, :].bitcast(F32), ALU.subtract).then_inc(shl_done, 1)
                g, i = divmod(n - 1 - SC - 1, SC)
                if n - 1 - SC - 1 >= 0 and i < GT and g < NG:
                    shared_add(GT * g + i)

            def shared_add(t):
                dve.wait_ge(sdn_done, t + 1)
                nc.vector.tensor_tensor(x_all[:, t, :], s_dn[t % 2], x_all[:, t, :], ALU.add).then_inc(sacc_done, 1)

            def expert_low(n):
                dve.wait_ge(ew_high, n + 1)
                nc.vector.tensor_tensor(pieces[n][1], stage(n), pieces[n][0].bitcast(F32),
                                        ALU.subtract).then_inc(ew_low, 1)

            for p in STEPS:
                if live(p - 1):
                    n_sum = inverse_sums(p - 1)
                if live(p - 2):
                    add_attention(p - 2)
                if live(p - 1):
                    values(p - 1, n_sum)
                if live(p - 2):
                    n_st2 = stats_2(p - 2)
                if live(p + 1):
                    norm_1(p + 1)
                if live(p - 2):
                    n_st2 = aggregate(mv2[:, p % 2, :], stats2[:, p % 2, :], n_st2)
                if live(p - 3):
                    z_low(p - 3)
                if live(p - 2):
                    plus_eps(mv2[:, p % 2, :], n_st2, var2_done)
                if live(p):
                    n_max = maxima(p, 0)
                if live(p + 2):
                    n_st1 = stats_1(p + 2)
                if live(p):
                    negated(p, 0, n_max)
                    n_max = maxima(p, 1)
                if live(p + 2):
                    n_st1 = aggregate(mv[:, p % 2, :], stats[:, p % 2, :], n_st1)
                if live(p):
                    negated(p, 1, n_max)
                if live(p - 2):
                    norm_2(p - 2)
                if live(p + 2):
                    plus_eps(mv[:, p % 2, :], n_st1, var_done)
                if p == 1:
                    dve.wait_ge(const_done, 7)
                if live(p - 4) and (p - 4) % RB == RB - 1 and p < NT + 3:
                    route((p - 4) // RB)
                if p == NT + 2:
                    route(NT // RB - 1)
                    destinations()
                for n in pieces_in(p):
                    shared_piece(n)
            done = 0
            for i, n in enumerate(REST):
                shared_piece(n)
                if i == 0:
                    table_and_weights()
                upto = (i + 1) * NP // len(REST)
                for w in range(done, upto):
                    expert_low(w)
                done = upto
            shared_add(NT - 1)
            dve.wait_ge(sc_done, B2 * NT)
            nc.vector.memset(hm[:, :, H:D], 0.0).then_inc(hm_pad, 1)

            for s in ESTEPS:
                if slot(s):
                    dve.wait_ge(exh_done, s + 1)
                    nc.vector.tensor_tensor(xl[:, s % 2, :], e_xt, xh[:, s % 2, :].bitcast(F32),
                                            ALU.subtract).then_inc(exl_done, 1)
                    dve.wait_ge(xs_in[s % 3], 16 * (s // 3 + 1))
                    nc.vector.scalar_tensor_tensor(yi[:, s:s + 1], xs[s % 3][:, D + 1:D + 2], slotno[:, s:s + 1],
                                                   xs[s % 3][:, D:D + 1], ALU.is_equal, ALU.add).then_inc(yi_done, 1)
                if slot(s - 1):
                    t = s - 1
                    dve.wait_ge(esg_done, t + 1)
                    if t >= 2:
                        dve.wait_ge(eht_done, t - 1)
                    nc.vector.tensor_tensor(hm[:, t % 2, 0:H], esg[t % 2], e_gu[t % 2][:, H:2 * H],
                                            ALU.mult).then_inc(ehm_done, 1)
                if slot(s - 2):
                    t = s - 2
                    dve.wait_ge(ehh_done, t + 1)
                    nc.vector.tensor_tensor(hl[:, t % 2, :], e_ht, hh[:, t % 2, :].bitcast(F32),
                                            ALU.subtract).then_inc(ehl_done, 1)

            for t in range(NT):
                dve.wait_ge(yk_in[t % 4], 16 * (t // 4 + 1))
                for k in range(K):
                    y = att_flat[:, ((t % 4) * K + k) * D:((t % 4) * K + k + 1) * D]
                    ins = nc.vector.scalar_tensor_tensor(x_all[:, t, :], y, wk[:, k, t:t + 1], x_all[:, t, :],
                                                         ALU.mult, ALU.add)
                    if k == 0:
                        link(ins)
                    else:
                        ins.then_inc(fin_done, 1)

        @block.tensor
        def _(pe):
            mm = nc.tensor.matmul

            def three(o, parts):
                for n, (ah, al, bh, bl) in enumerate(parts):
                    mm(o, ah, bh, start=(n == 0), stop=False)
                    mm(o, ah, bl, start=False, stop=False)
                    last = mm(o, al, bh, start=False, stop=(n == len(parts) - 1))
                return last

            def scores(k):
                j = k % 2
                pe.wait_ge(kq_low, k + 1)
                if k >= 2:
                    pe.wait_ge(exp_done, B2 * (k - 1))
                for b in range(B2):
                    r = slice(b * S, (b + 1) * S)
                    for c in range(DC):
                        e = slice(c * P, (c + 1) * P)
                        last = three(ps_s[j][b][:, c * D:(c + 1) * D],
                                     [(kh[r, j, e], kl[r, j, e], qh[r, j, :], ql[r, j, :])])
                    last.then_inc(sc_done, 1)

            def context_T(k):
                if k >= 1:
                    pe.wait_ge(vt_done, k)
                pe.wait_ge(c_in[k % NL], 16 * (k // NL + 1))
                for c in range(DC):
                    last = nc.tensor.transpose(ps_c[:, c * P:(c + 1) * P], cr[:, k % NL, c * P:(c + 1) * P], ident[:])
                last.then_inc(ct_done, 1)

            def attend(k):
                j = k % 2
                pe.wait_ge(vt_done, k + 1)
                if k >= 1:
                    pe.wait_ge(x1_done, k)
                for b in range(B2):
                    for c in range(DC):
                        m = (b * DC + c) * D
                        last = mm(ps_o[b * S:(b + 1) * S, :], vT[:, j, c, b, :], att[:, j, m:m + D],
                                  start=(c == 0), stop=(c == DC - 1))
                last.then_inc(out_done, 1)

            def z_T(k):
                pe.wait_ge(z_done, k + 1)
                if k >= 1:
                    pe.wait_ge(el_done, k)
                for c in range(DC):
                    last = nc.tensor.transpose(zT[:, c * P:(c + 1) * P], z_all[:, k, c * P:(c + 1) * P], ident[:])
                last.then_inc(zt_done, 1)

            def route_logits(k):
                pe.wait_ge(zl_done, k + 1)
                if k == 0:
                    pe.wait_ge(gw_done, 1)
                t = slice(k * P, (k + 1) * P)
                three(logits, [(zTh[:, c, t], zTl[:, c, t], gwh[:, c * E:(c + 1) * E], gwl[:, c * E:(c + 1) * E])
                               for c in range(DC)]).then_inc(lg_done, 1)

            def ranks(r):
                pe.wait_ge(both_done, r + 1)
                for t in range(r * RB, (r + 1) * RB):
                    mm(rank[:, t * E:(t + 1) * E], below[:], both[:, t, :], start=(t == 0), stop=False,
                       skip_group_check=True)
                    n = NT - t
                    last = mm(rank[:, (t + 1) * E:(NT + 1) * E], ones[:],
                              both[:, t:t + 1, :].broadcast_to([P, n, E]), start=False, stop=(t == NT - 1),
                              skip_group_check=True)
                if r == NT // RB - 1:
                    last.then_inc(rank_done, 1)

            def shared_up(g, c):
                n, m = SC * g + c, CHUNK[c]
                if n == 0:
                    pe.wait_ge(sw_low, DC + 1)
                    pe.wait_ge(exp_done, B2 * NT)
                if n >= 3:
                    pe.wait_ge(shm_done, n - 2)
                if c == 0:
                    pe.wait_ge(zl_done, GT * (g + 1))
                t = slice(g * GN, (g + 1) * GN)
                for h in range(2):
                    f = slice(h * HS + c * P, h * HS + c * P + m)
                    last = three(s_gu[n % 3][0:m, h * GN:(h + 1) * GN],
                                 [(suh[:, d, f], sul[:, d, f], zTh[:, d, t], zTl[:, d, t]) for d in range(DC)])
                last.then_inc(sup_done, 1)

            def shared_down(g, i):
                t = GT * g + i
                pe.wait_ge(shl_done, SC * (g + 1))
                if t >= 2:
                    pe.wait_ge(sacc_done, t - 1)
                if t == 1:
                    pe.wait_ge(vt_done, NT)
                s = slice(i * P, (i + 1) * P)
                three(s_dn[t % 2], [(s_hh[0:m, g % 2, c, s], s_hl[0:m, g % 2, c, s], sdh[0:m, c, :], sdl[0:m, c, :])
                                    for c, m in enumerate(CHUNK)]).then_inc(sdn_done, 1)

            def shared_piece(n):
                if n < NPC:
                    shared_up(n // SC, n % SC)
                g, i = divmod(n - SC - 1, SC)
                if n - SC - 1 >= 0 and i < GT and g < NG:
                    shared_down(g, i)

            pe.wait_ge(id_done, 1)
            for p in STEPS:
                if live(p):
                    scores(p)
                if live(p - 3):
                    route_logits(p - 3)
                if live(p):
                    context_T(p)
                if live(p - 1):
                    attend(p - 1)
                if live(p - 2):
                    z_T(p - 2)
                if p == 3:
                    pe.wait_ge(const_done, 7)
                if live(p - 4) and (p - 4) % RB == RB - 1 and p < NT + 3:
                    ranks((p - 4) // RB)
                if p == NT + 2:
                    ranks(NT // RB - 1)
                for n in pieces_in(p):
                    shared_piece(n)
            for n in REST:
                shared_piece(n)

            pe.wait_ge(tab_done, 1)
            pe.wait_ge(ew_low, NP)
            pe.wait_ge(hm_pad, 1)
            for s in ESTEPS:
                if slot(s):
                    pe.wait_ge(xs_in[s % 3], 16 * (s // 3 + 1))
                    if s >= 1:
                        pe.wait_ge(exl_done, s)
                    for c in range(DC):
                        last = nc.tensor.transpose(e_xt[:, c * P:(c + 1) * P], xs[s % 3][:, c * P:(c + 1) * P], ident[:])
                    last.then_inc(ext_done, 1)
                if slot(s - 1):
                    t, j = s - 1, (s - 1) % 2
                    expert = pe.value_load(tab[0:1, t:t + 1], min_val=0, max_val=E - 1)
                    pe.wait_ge(exl_done, t + 1)
                    if t >= 2:
                        pe.wait_ge(ehm_done, t - 1)
                    o = e_gu[j][:, 0:2 * H]
                    w = [[b[:, bass.ds(expert, 1), c * 2 * H:(c + 1) * 2 * H].rearrange("p a f -> p (a f)")
                          for b in (uph, upl)] for c in range(DC)]
                    three(o, [(xh[:, j, c * P:(c + 1) * P], xl[:, j, c * P:(c + 1) * P], w[c][0], w[c][1])
                              for c in range(DC)]).then_inc(eup_done, 1)
                if slot(s - 2):
                    t = s - 2
                    pe.wait_ge(ehm_done, t + 1)
                    if t >= 1:
                        pe.wait_ge(ehl_done, t)
                    for c in range(DC):
                        last = nc.tensor.transpose(e_ht[:, c * P:(c + 1) * P], hm[:, t % 2, c * P:(c + 1) * P], ident[:])
                    last.then_inc(eht_done, 1)
                if slot(s - 3):
                    t, j = s - 3, (s - 3) % 2
                    expert = pe.value_load(tab[0:1, t:t + 1], min_val=0, max_val=E - 1)
                    pe.wait_ge(ehl_done, t + 1)
                    if t >= 2:
                        pe.wait_ge(ey_done, t - 1)
                    w = [[b[:, bass.ds(expert, 1), c * D:(c + 1) * D].rearrange("p a f -> p (a f)")
                          for b in (dnh, dnl)] for c in range(DC)]
                    three(e_y[j], [(hh[:, j, c * P:(c + 1) * P], hl[:, j, c * P:(c + 1) * P], w[c][0], w[c][1])
                                   for c in range(DC)]).then_inc(edn_done, 1)


def kernel(x, ctx_2048, L0_ffn_gate_w, L0_ffn_gate_bias, L0_ffn_shared_gw, L0_ffn_shared_dw, L0_ffn_up_w,
           L0_ffn_down_w):
    import numpy as np
    import concourse.bacc as bacc
    from concourse.bass_utils import run_bass_kernel_spmd

    x, ctx_kv = np.asarray(x), np.asarray(ctx_2048)
    up_w, down_w = np.asarray(L0_ffn_up_w), np.asarray(L0_ffn_down_w)
    sgw, sdw = np.asarray(L0_ffn_shared_gw), np.asarray(L0_ffn_shared_dw)
    P = 128
    E, D, H = down_w.shape
    HS = sdw.shape[1]
    DC, SC = D // P, -(-HS // P)
    up_wT = np.ascontiguousarray(up_w.transpose(2, 0, 1).reshape(DC, P, E, 2 * H).transpose(1, 2, 0, 3))
    down_wT = np.zeros((P, E, DC, D), x.dtype)
    for c in range(DC):
        h = down_w[:, :, c * P:min(H, (c + 1) * P)]
        down_wT[0:h.shape[2], :, c, :] = h.transpose(2, 0, 1)
    su = np.concatenate([sgw[HS:], sgw[:HS]]).T
    shared_upT = np.ascontiguousarray(su.reshape(DC, P, 2 * HS).transpose(1, 0, 2))
    shared_dnT = np.zeros((P, SC, D), x.dtype)
    for c in range(SC):
        h = sdw[:, c * P:min(HS, (c + 1) * P)]
        shared_dnT[0:h.shape[1], c, :] = h.T
    gate = np.ascontiguousarray(np.asarray(L0_ffn_gate_w).T.reshape(DC, P, E).transpose(1, 0, 2)).reshape(P, DC * E)
    gbias = np.ascontiguousarray(np.broadcast_to(np.asarray(L0_ffn_gate_bias), (P, E)))
    arrays = {"x": x.reshape(-1, D), "ctx_kv": ctx_kv.reshape(-1, D), "up_wT": up_wT.reshape(P, E, -1),
              "down_wT": down_wT.reshape(P, E, -1), "shared_upT": shared_upT, "shared_dnT": shared_dnT,
              "gate_wT": gate, "gate_bias": gbias}
    nc = bacc.Bacc("TRN2", target_bir_lowering=False, num_devices=1)
    aps = {n: nc.dram_tensor(n, a.shape, mybir.dt.from_np(a.dtype), kind="ExternalInput").ap()
           for n, a in arrays.items()}
    out = nc.dram_tensor("out", arrays["x"].shape, mybir.dt.float32, kind="ExternalOutput").ap()
    xattn_moe_kernel(nc, *aps.values(), out)
    r = run_bass_kernel_spmd(nc, [{n: np.ascontiguousarray(a) for n, a in arrays.items()}], core_ids=[0])
    return r.results[0]["out"].reshape(x.shape)
```

```python
import concourse.bass as bass
from concourse import mybir
from contextlib import ExitStack


def xattn_moe_kernel(nc, x, ctx_kv, up_wT, down_wT, shared_upT, shared_dnT, gate_wT, gate_bias, out):
    F32, F32R, BF16 = mybir.dt.float32, mybir.dt.float32r, mybir.dt.bfloat16
    U32, I32 = mybir.dt.uint32, mybir.dt.int32
    ALU, ACT, AX = mybir.AluOpType, mybir.ActivationFunctionType, mybir.AxisListType

    P = 128
    TOK, D = x.shape
    S = 64
    B2 = P // S
    NT = TOK // P
    DC = D // P
    E = up_wT.shape[1]
    K = 2
    H = up_wT.shape[2] // (2 * DC)
    HS = shared_upT.shape[2] // 2
    SC = -(-HS // P)
    CHUNK = [min(P, HS - c * P) for c in range(SC)]
    SLOTS = (K * TOK + E * (P - 1)) // P
    ROW = D + 2
    TRASH = K * TOK
    SCALE = float(D) ** -0.5
    EPS = 1e-5
    GT = 2
    GN = GT * P
    NG = NT // GT
    RB = 4
    NL = 4
    PADS = -(-SLOTS // (NT - NL))

    slot_rows = nc.dram_tensor("slot_rows", [SLOTS * P, ROW], F32, kind="Internal").ap()
    expert_out = nc.dram_tensor("expert_out", [TRASH + SLOTS * P, D], F32, kind="Internal").ap()

    with ExitStack() as stack:
        def sb(name, shape, dt=F32):
            return stack.enter_context(nc.sbuf_tensor(name, shape, dt))

        def sem(name):
            return stack.enter_context(nc.semaphore(name))

        bank = [stack.enter_context(nc.psum_tensor(f"bank{i}", [P, 512], F32)) for i in range(8)]

        x_all = sb("x_all", [P, NT, D])
        z_all = sb("z_all", [P, NT, ROW])
        zTh = sb("zTh", [P, DC, TOK], F32R)
        zTl = sb("zTl", [P, DC, TOK], F32R)
        uph = sb("uph", [P, E, DC * 2 * H], F32R)
        upl = sb("upl", [P, E, DC * 2 * H], F32R)
        dnh = sb("dnh", [P, E, DC * D], F32R)
        dnl = sb("dnl", [P, E, DC * D], F32R)
        suh = sb("suh", [P, DC, 2 * HS], F32R)
        sul = sb("sul", [P, DC, 2 * HS], F32R)
        sdh = sb("sdh", [P, SC, D], F32R)
        sdl = sb("sdl", [P, SC, D], F32R)
        gws = sb("gws", [P, DC * E])
        gwh = sb("gwh", [P, DC * E], F32R)
        gwl = sb("gwl", [P, DC * E], F32R)
        bias = sb("bias", [P, E])
        cr = sb("cr", [P, NL, D])
        q = sb("q", [P, 2, D])
        kh = sb("kh", [P, 2, D], F32R)
        kl = sb("kl", [P, 2, D], F32R)
        qh = sb("qh", [P, 2, D], F32R)
        ql = sb("ql", [P, 2, D], F32R)
        att = sb("att", [P, 2, B2 * DC * D])
        vT = sb("vT", [P, 2, DC, B2, S])
        stats = sb("stats", [P, 2, 6])
        mv = sb("mv", [P, 2, 2])
        rstd = sb("rstd", [P, 2, 1])
        stats2 = sb("stats2", [P, 2, 6])
        mv2 = sb("mv2", [P, 2, 2])
        rstd2 = sb("rstd2", [P, 2, 1])
        nb = sb("nb", [P, 2, DC * B2])
        rs = sb("rs", [P, 2, DC * B2])
        ri = sb("ri", [P, 2, DC * B2])
        ident = sb("ident", [P, P])
        below = sb("below", [P, P], BF16)
        ones = sb("ones", [P, P], BF16)
        mhalf = sb("mhalf", [P, 1])
        iota_e = sb("iota_e", [P, E])
        lower = sb("lower", [P, E, E])
        iota_n = sb("iota_n", [P, NT])
        slotno = sb("slotno", [P, SLOTS])
        tileno = sb("tileno", [1, SLOTS])
        no_token = sb("no_token", [P, D])
        no_place = sb("no_place", [P, SLOTS, 2])
        el = sb("el", [P, NT, E])
        sg = sb("sg", [P, NT, E])
        sbias = sb("sbias", [P, NT, E])
        top = sb("top", [P, NT, E])
        tidx = sb("tidx", [P, NT, E], U32)
        fidx = sb("fidx", [P, NT, K])
        pick = sb("pick", [P, K, NT, E])
        both = sb("both", [P, NT, E], BF16)
        wk = sb("wk", [P, K, NT])
        wsum = sb("wsum", [P, 2, NT])
        big = sb("big", [P, E, NT])
        small = sb("small", [P, 4, E])
        tri = sb("tri", [P, E, E])
        dest = sb("dest", [P, K, NT])
        desti = sb("desti", [P, K, NT], U32)
        cmp_t = sb("cmp_t", [1, SLOTS, E])
        tab_f = sb("tab_f", [1, SLOTS])
        tab = sb("tab", [1, SLOTS], I32)
        s_sg = sb("s_sg", [P, 2, GN])
        s_hm = sb("s_hm", [P, 2, GN])
        s_hh = sb("s_hh", [P, 2, SC, GN], F32R)
        s_hl = sb("s_hl", [P, 2, SC, GN], F32R)
        yi = sb("yi", [P, SLOTS], U32)

        z_flat = z_all[:, :, :].rearrange("p t c -> p (t c)")
        SU, SD = DC * 2 * HS, SC * D
        SRAW = NT * ROW - SU - SD
        su_raw = z_flat[:, SRAW:SRAW + SU]
        sd_raw = z_flat[:, SRAW + SU:SRAW + SU + SD]
        FIRST_RAW = SRAW // ROW
        att_flat = att[:, :, :].rearrange("p j c -> p (j c)")
        cr_flat = cr[:, :, :].rearrange("p j d -> p (j d)")
        xs = [cr_flat[:, i * ROW:(i + 1) * ROW] for i in range(3)]
        ys = [att_flat[:, 3 * ROW + i * D:3 * ROW + (i + 1) * D] for i in range(3)]
        esg = [att_flat[:, 3 * (ROW + D) + i * H:3 * (ROW + D) + (i + 1) * H] for i in range(2)]
        xh, xl, hh, hl, hm = kh, kl, qh, ql, q

        ps_s = [[bank[0], bank[1]], [bank[2], bank[3]]]
        ps_c, ps_o = bank[4][:, 0:D], bank[5][:, 0:D]
        zT, logits = bank[6][:, 0:D], bank[6][:, D:D + E]
        rank = bank[7][:, 0:(NT + 1) * E]
        s_gu = [bank[0], bank[1], bank[2]]
        s_dn = [bank[3][:, 0:D], bank[4][:, 0:D]]
        e_xt = [bank[6][:, 0:D], bank[3][:, 0:D]]
        e_gu = [bank[0], bank[1]]
        e_ht = [bank[5][:, 0:D], bank[4][:, 0:D]]
        e_y = [bank[7][:, 0:D], bank[2][:, 0:D]]

        x_in = [sem(f"x_in{i}") for i in range(NL)]
        c_in = [sem(f"c_in{i}") for i in range(NL)]
        g_in, sw_in, pads_in = sem("g_in"), sem("sw_in"), sem("pads_in")
        ew_in = [sem("up_in0"), sem("up_in1"), sem("down_in")]
        const_done = sem("const_done")
        id_done = sem("id_done")
        pad_row = sem("pad_row")
        ztail_done = sem("ztail_done")
        var_done, rstd_done, q_done = sem("var_done"), sem("rstd_done"), sem("q_done")
        kq_high, kq_low = sem("kq_high"), sem("kq_low")
        sc_done, ct_done, nb_done, exp_done = sem("sc_done"), sem("ct_done"), sem("nb_done"), sem("exp_done")
        vt_done, out_done, x1_done = sem("vt_done"), sem("out_done"), sem("x1_done")
        var2_done, rstd2_done, z_done = sem("var2_done"), sem("rstd2_done"), sem("z_done")
        zt_done, zh_done, zl_done = sem("zt_done"), sem("zh_done"), sem("zl_done")
        lg_done, el_done = sem("lg_done"), sem("el_done")
        gw_done, sw_high, sw_low = sem("gw_done"), sem("sw_high"), sem("sw_low")
        ew_high, ew_low = sem("ew_high"), sem("ew_low")
        both_done, rank_done = sem("both_done"), sem("rank_done")
        dest_done, tab_done, sent = sem("dest_done"), sem("tab_done"), sem("sent")
        sup_done, ssg_done, shm_done = sem("sup_done"), sem("ssg_done"), sem("shm_done")
        shh_done, shl_done, sdn_done, sacc_done = sem("shh_done"), sem("shl_done"), sem("sdn_done"), sem("sacc_done")
        xs_in = [sem(f"xs_in{i}") for i in range(3)]
        yi_done = sem("yi_done")
        ext_done, exh_done, exl_done = sem("ext_done"), sem("exh_done"), sem("exl_done")
        eup_done, esg_done, ehm_done = sem("eup_done"), sem("esg_done"), sem("ehm_done")
        eht_done, ehh_done, ehl_done = sem("eht_done"), sem("ehh_done"), sem("ehl_done")
        edn_done, ey_done = sem("edn_done"), sem("ey_done")
        y_out = [sem(f"y_out{i}") for i in range(3)]
        yk_in = [sem(f"yk_in{i}") for i in range(4)]
        y0_done, y1_done, fin_done = sem("y0_done"), sem("y1_done"), sem("fin_done")
        hm_pad = sem("hm_pad")
        stored = sem("stored")
        c_dve = sem("c_dve")
        c_pool = sem("c_pool")

        block = stack.enter_context(nc.Block())

        STEPS = range(-2, NT + 4)

        def live(t):
            return 0 <= t < NT

        WARM = 10
        FILL = 3

        PIECES = range(NG * SC + SC)
        PAUSE = SC * (NG - 3) + 1
        EARLY, LATE = range(PAUSE), range(PAUSE, len(PIECES))
        AHEAD = range(NT, NT + 3)

        TAILS = 2

        def tails_after(n):
            i = n - PAUSE - 3
            return range(min(TAILS * i, NT - GT), min(TAILS * (i + 1), NT - GT)) if i >= 0 else range(0)

        pieces = [part for e in range(E) for part in ((uph[:, e, :], upl[:, e, :], up_wT[:, e, :]),
                                                      (dnh[:, e, :], dnl[:, e, :], down_wT[:, e, :]))]
        NP = len(pieces)
        assert NP <= PAUSE

        def stage(n):
            e, down = divmod(n, 2)
            start = 2 * DC * 2 * H if down else e % 2 * DC * 2 * H
            return att_flat[:, start:start + pieces[n][2].shape[1]]

        def staged(n):
            e, down = divmod(n, 2)
            return (ew_in[2], 16 * (e + 1)) if down else (ew_in[e % 2], 16 * (e // 2 + 1))

        ESTEPS = range(SLOTS + 3)

        def slot(t):
            return 0 <= t < SLOTS

        @block.sync
        def _(sp):
            xv = x.rearrange("(t p) d -> t p d", p=P)
            cv = ctx_kv.rearrange("(t p) d -> t p d", p=P)

            def load(p):
                j = p % NL
                if p >= NL:
                    sp.wait_ge(x_in[j], 16 * (p // NL))
                sp.dma_start(x_all[:, p, :], xv[p]).then_inc(x_in[j], 16)
                if p >= NL:
                    sp.wait_ge(kq_low, p - NL + 1)
                    sp.wait_ge(ct_done, p - NL + 1)
                sp.dma_start(cr[:, j, :], cv[p]).then_inc(c_in[j], 16)

            load(0)
            load(1)
            load(2)
            load(3)
            sp.dma_start(gws[:], gate_wT).then_inc(g_in, 16)
            sp.dma_start(bias[:], gate_bias).then_inc(g_in, 16)
            sp.dma_start(su_raw, shared_upT.rearrange("p c f -> p (c f)")).then_inc(sw_in, 16)
            sp.dma_start(sd_raw, shared_dnT.rearrange("p c f -> p (c f)")).then_inc(sw_in, 16)
            sp.wait_ge(pad_row, 3)
            rows = slot_rows.rearrange("(t p) c -> p t c", p=P)
            for p in range(NL, NT):
                load(p)
                t = slice((p - NL) * PADS, min(SLOTS, (p - NL + 1) * PADS))
                n = t.stop - t.start
                if n > 0:
                    sp.dma_start(rows[:, t, 0:D], no_token[:, :].unsqueeze(1).broadcast_to([P, n, D])).then_inc(pads_in, 16)
                    sp.dma_start(rows[:, t, D:ROW], no_place[:, t, :]).then_inc(pads_in, 16)
            sp.wait_ge(out_done, NT)
            for n in range(NP):
                before = n - 2 if n % 2 else n - 4
                if before >= 0:
                    sp.wait_ge(ew_low, before + 1)
                sp.dma_start(stage(n), pieces[n][2]).then_inc(staged(n)[0], 16)
            sp.wait_ge(ct_done, NT)
            sp.wait_ge(kq_low, NT)
            sp.wait_ge(sent, 16 * K * NT)
            sv = slot_rows.rearrange("(t p) c -> t p c", p=P)
            for t in range(SLOTS):
                if t >= 3:
                    sp.wait_ge(ext_done, t - 2)
                    sp.wait_ge(yi_done, t - 2)
                sp.dma_start(xs[t % 3], sv[t]).then_inc(xs_in[t % 3], 16)
            for i in range(3):
                sp.wait_ge(y_out[i], 16 * len(range(i, SLOTS, 3)))
            yv = expert_out[0:TRASH, :].rearrange("(t p k) d -> t p (k d)", p=P, k=K)
            ov = out.rearrange("(t p) d -> t p d", p=P)
            for t in range(NT + 4):
                if t >= 4:
                    sp.wait_ge(fin_done, t - 3)
                if t < NT:
                    sp.dma_start(att_flat[:, (t % 4) * K * D:(t % 4 + 1) * K * D], yv[t]).then_inc(yk_in[t % 4], 16)
                if t >= 4:
                    sp.dma_start(ov[t - 4], x_all[:, t - 4, :]).then_inc(stored, 16)
            sp.wait_ge(stored, 16 * NT)

        @block.gpsimd
        def _(pool):
            def iota(ap, pattern, base, mult):
                return nc.gpsimd.iota(ap, pattern, base=base, channel_multiplier=mult,
                                      allow_small_or_imprecise_dtypes=True)

            nc.gpsimd.memset(mhalf[:], -0.5)
            nc.gpsimd.memset(ident[:], 0.0).then_inc(c_pool, 1)
            pool.wait_ge(c_pool, 1)
            nc.gpsimd.affine_select(out=ident[:], in_=ident[:], compare_op=ALU.not_equal, fill=1.0,
                                    base=0, pattern=[[-1, P]], channel_multiplier=1).then_inc(id_done, 1)
            n_pool = [1]

            def prepare():
                nc.gpsimd.memset(no_token[:], 0.0).then_inc(pad_row, 1)
                iota(no_place[:, :, 0], [[P, SLOTS]], TRASH, 1).then_inc(pad_row, 1)
                nc.gpsimd.memset(no_place[:, :, 1], -1.0).then_inc(pad_row, 1)
                iota(iota_e[:], [[1, E]], 0, 0).then_inc(const_done, 1)
                iota(iota_n[:], [[P, NT]], 0, 0).then_inc(const_done, 1)
                iota(slotno[:], [[P, SLOTS]], 0, 1).then_inc(const_done, 1)
                iota(tileno[:], [[1, SLOTS]], 0, 0).then_inc(const_done, 1)
                nc.gpsimd.memset(ones[:], 1.0).then_inc(const_done, 1)
                nc.gpsimd.memset(below[:], 1.0).then_inc(c_pool, 1)
                nc.gpsimd.memset(lower[:], 1.0).then_inc(c_pool, 1)
                n_pool[0] += 2
                pool.wait_ge(c_pool, n_pool[0])
                nc.gpsimd.affine_select(out=below[:], in_=below[:], compare_op=ALU.is_gt, fill=0.0,
                                        base=0, pattern=[[1, P]], channel_multiplier=-1).then_inc(const_done, 1)
                nc.gpsimd.affine_select(out=lower[:], in_=lower[:], compare_op=ALU.is_gt, fill=0.0,
                                        base=0, pattern=[[1, E], [-1, E]], channel_multiplier=0).then_inc(const_done, 1)

            def gate_split():
                pool.wait_ge(g_in, 32)
                nc.gpsimd.tensor_copy(gwh[:], gws[:]).then_inc(c_pool, 1)
                n_pool[0] += 1
                pool.wait_ge(c_pool, n_pool[0])
                nc.gpsimd.tensor_tensor(gwl[:], gws[:], gwh[:].bitcast(F32), ALU.subtract).then_inc(gw_done, 1)

            def shared_low(piece):
                pool.wait_ge(sw_high, piece + 1)
                if piece < DC:
                    r = slice(piece * 2 * HS, (piece + 1) * 2 * HS)
                    nc.gpsimd.tensor_tensor(sul[:, piece, :], su_raw[:, r], suh[:, piece, :].bitcast(F32),
                                            ALU.subtract).then_inc(sw_low, 1)
                else:
                    nc.gpsimd.tensor_tensor(sdl[:, :, :].rearrange("p c d -> p (c d)"), sd_raw,
                                            sdh[:, :, :].rearrange("p c d -> p (c d)").bitcast(F32),
                                            ALU.subtract).then_inc(sw_low, 1)

            for p in STEPS:
                if live(p - 2):
                    k, j = p - 2, p % 2
                    pool.wait_ge(var2_done, k + 1)
                    nc.gpsimd.tensor_tensor(rstd2[:, j, :], mv2[:, j, 1:2], mhalf[:], ALU.pow).then_inc(rstd2_done, 1)
                if live(p + 1):
                    k, j = p + 1, (p + 1) % 2
                    if k >= 2:
                        pool.wait_ge(sc_done, B2 * (k - 1))
                    pool.wait_ge(kq_high, 2 * k + 1)
                    nc.gpsimd.tensor_tensor(kl[:, j, :], cr[:, k % NL, :], kh[:, j, :].bitcast(F32), ALU.subtract)
                    pool.wait_ge(kq_high, 2 * k + 2)
                    nc.gpsimd.tensor_tensor(ql[:, j, :], q[:, j, :], qh[:, j, :].bitcast(F32),
                                            ALU.subtract).then_inc(kq_low, 1)
                if live(p + 2):
                    k, j = p + 2, p % 2
                    pool.wait_ge(var_done, k + 1)
                    nc.gpsimd.tensor_tensor(rstd[:, j, :], mv[:, j, 1:2], mhalf[:], ALU.pow).then_inc(rstd_done, 1)
                if p == -2:
                    prepare()
                if p == -1:
                    gate_split()
                if 1 <= p < DC + 2:
                    shared_low(p - 1)
                if p == DC + 2:
                    pool.wait_ge(sw_low, DC + 1)
                    iota(z_all[:, :, D], [[2 * P, NT]], 0, 2).then_inc(ztail_done, 1)

            pool.wait_ge(dest_done, 2)
            pool.wait_ge(ztail_done, 1)
            pool.wait_ge(z_done, NT)
            pool.wait_ge(pads_in, 32 * -(-SLOTS // PADS))
            for k in range(K):
                for t in range(NT):
                    nc.gpsimd.indirect_dma_start(
                        slot_rows, bass.IndirectOffsetOnAxis(ap=desti[:, k, t:t + 1], axis=0),
                        z_all[:, t, :], None).then_inc(sent, 16)
            for t in range(SLOTS):
                pool.wait_ge(ey_done, t + 1)
                pool.wait_ge(yi_done, t + 1)
                nc.gpsimd.indirect_dma_start(
                    expert_out, bass.IndirectOffsetOnAxis(ap=yi[:, t:t + 1], axis=0),
                    ys[t % 3], None).then_inc(y_out[t % 3], 16)
            for t in range(NT):
                pool.wait_ge(y1_done, t + 1)
                pool.wait_ge(y0_done, t + 1)
                nc.gpsimd.tensor_tensor(x_all[:, t, :], x_all[:, t, :],
                                        att_flat[:, ((t % 4) * K + 1) * D:((t % 4) * K + 2) * D],
                                        ALU.add).then_inc(fin_done, 1)

        @block.scalar
        def _(act):
            def copy(o, i):
                return nc.scalar.activation(o, i, ACT.Copy)

            def shared_high(piece):
                if piece == 0:
                    act.wait_ge(sw_in, 32)
                if piece < DC:
                    copy(suh[:, piece, :], su_raw[:, piece * 2 * HS:(piece + 1) * 2 * HS]).then_inc(sw_high, 1)
                else:
                    copy(sdh[:, :, :].rearrange("p c d -> p (c d)"), sd_raw).then_inc(sw_high, 1)

            def shared_piece(n):
                if n < NG * SC:
                    m = CHUNK[n % SC]
                    act.wait_ge(sup_done, n + 1)
                    if n >= 2:
                        act.wait_ge(shm_done, n - 1)
                    nc.scalar.activation(s_sg[0:m, n % 2, :], s_gu[n % 3][0:m, 0:GN], ACT.Silu).then_inc(ssg_done, 1)
                if 0 <= n - 1 < NG * SC:
                    g, c = (n - 1) // SC, (n - 1) % SC
                    m = CHUNK[c]
                    if c == 0 and g >= 2:
                        act.wait_ge(sdn_done, GT * (g - 1))
                    act.wait_ge(shm_done, n)
                    copy(s_hh[0:m, g % 2, c, :], s_hm[0:m, (n - 1) % 2, :]).then_inc(shh_done, 1)

            def expert_high(n):
                act.wait_ge(*staged(n))
                copy(pieces[n][0], stage(n)).then_inc(ew_high, 1)

            for p in STEPS:
                if live(p + 1):
                    k, j = p + 1, (p + 1) % 2
                    act.wait_ge(c_in[k % NL], 16 * (k // NL + 1))
                    if k >= 2:
                        act.wait_ge(sc_done, B2 * (k - 1))
                    copy(kh[:, j, :], cr[:, k % NL, :]).then_inc(kq_high, 1)
                    act.wait_ge(q_done, k + 1)
                    copy(qh[:, j, :], q[:, j, :]).then_inc(kq_high, 1)
                for b in range(B2):
                    if live(p):
                        k, j = p, p % 2
                        if k >= 2:
                            act.wait_ge(out_done, k - 1)
                        act.wait_ge(nb_done, B2 * k + b + 1)
                        for c in range(DC):
                            n = c * B2 + b
                            m = (b * DC + c) * D
                            last = nc.scalar.activation(att[:, j, m:m + D], ps_s[j][b][:, c * D:(c + 1) * D],
                                                        ACT.Exp, bias=nb[:, j, n:n + 1],
                                                        accum_out=rs[:, j, n:n + 1])
                        last.then_inc(exp_done, 1)
                    if b == 0 and live(p - 3):
                        act.wait_ge(lg_done, p - 2)
                        nc.scalar.activation(el[:, p - 3, :], logits, ACT.Exp, scale=-1.0).then_inc(el_done, 1)
                if live(p - 2):
                    k = p - 2
                    act.wait_ge(zt_done, k + 1)
                    copy(zTh[:, :, k * P:(k + 1) * P], zT.rearrange("p (c t) -> p c t", c=DC)).then_inc(zh_done, 1)
                if 0 <= p < DC + 1:
                    shared_high(p)
            for n in EARLY:
                shared_piece(n)
                if n < NP:
                    expert_high(n)

            for s in ESTEPS:
                if slot(s):
                    act.wait_ge(ext_done, s + 1)
                    if s >= 2:
                        act.wait_ge(eup_done, s - 1)
                    copy(xh[:, s % 2, :], e_xt[s % 2]).then_inc(exh_done, 1)
                if slot(s - 1):
                    t = s - 1
                    act.wait_ge(eup_done, t + 1)
                    if t >= 2:
                        act.wait_ge(ehm_done, t - 1)
                    nc.scalar.activation(esg[t % 2], e_gu[t % 2][:, 0:H], ACT.Silu).then_inc(esg_done, 1)
                if slot(s - 2):
                    t = s - 2
                    act.wait_ge(eht_done, t + 1)
                    if t >= 2:
                        act.wait_ge(edn_done, t - 1)
                    copy(hh[:, t % 2, :], e_ht[t % 2]).then_inc(ehh_done, 1)
                if slot(s - 3):
                    t = s - 3
                    act.wait_ge(edn_done, t + 1)
                    if t >= 3:
                        act.wait_ge(y_out[t % 3], 16 * (t // 3))
                    copy(ys[t % 3], e_y[t % 2]).then_inc(ey_done, 1)

            def weigh_second(t):
                act.wait_ge(yk_in[t % 4], 16 * (t // 4 + 1))
                y = att_flat[:, ((t % 4) * K + 1) * D:((t % 4) * K + 2) * D]
                nc.scalar.activation(y, y, ACT.Copy, scale=wk[:, 1, t:t + 1]).then_inc(y1_done, 1)

            for n in LATE:
                shared_piece(n)
                for t in tails_after(n):
                    weigh_second(t)
            for t in range(tails_after(LATE[-1]).stop, NT):
                weigh_second(t)

        @block.vector
        def _(dve):
            chain = [0]

            def mark(ins):
                ins.then_inc(c_dve, 1)
                chain[0] += 1
                return chain[0]

            def link(ins):
                dve.wait_ge(c_dve, mark(ins))

            def stats_1(k):
                j = k % 2
                dve.wait_ge(x_in[k % NL], 16 * (k // NL + 1))
                return mark(nc.vector.bn_stats(stats[:, j, :], x_all[:, k, :]))

            def aggregate(m, st, n):
                dve.wait_ge(c_dve, n)
                return mark(nc.vector.bn_aggr(m, st))

            def plus_eps(m, n, done, scale):
                dve.wait_ge(c_dve, n)
                nc.vector.tensor_scalar(m[:, 1:2], m[:, 1:2], EPS, scale ** -2, ALU.add, ALU.mult).then_inc(done, 1)

            def norm_1(k):
                j = k % 2
                dve.wait_ge(rstd_done, k + 1)
                if k >= 2:
                    dve.wait_ge(kq_low, k - 1)
                nc.vector.tensor_scalar(q[:, j, :], x_all[:, k, :], mv[:, j, 0:1], rstd[:, j, :],
                                        ALU.subtract, ALU.mult).then_inc(q_done, 1)

            def maxima(k, b):
                j = k % 2
                if k >= 2:
                    dve.wait_ge(exp_done, B2 * (k - 1))
                m = nb[:, j, :].rearrange("p (c b) -> p b c", b=B2)
                dve.wait_ge(sc_done, B2 * k + b + 1)
                nc.vector.tensor_reduce(m[:, b, :], ps_s[j][b][:, :].rearrange("p (c d) -> p c d", c=DC),
                                        AX.X, ALU.max, negate=True).then_inc(nb_done, 1)

            def inverse_sums(k):
                dve.wait_ge(exp_done, B2 * (k + 1))
                return mark(nc.vector.reciprocal(ri[:, k % 2, :], rs[:, k % 2, :]))

            def values(k, n):
                j = k % 2
                dve.wait_ge(c_dve, n)
                dve.wait_ge(ct_done, k + 1)
                if k >= 2:
                    dve.wait_ge(out_done, k - 1)
                nc.vector.tensor_tensor(vT[:, j, :, :, :].rearrange("p c b s -> p (c b) s"),
                                        ps_c.rearrange("p (n s) -> p n s", s=S),
                                        ri[:, j, :].unsqueeze(2).broadcast_to([P, DC * B2, S]),
                                        ALU.mult).then_inc(vt_done, 1)

            def add_attention(k):
                dve.wait_ge(out_done, k + 1)
                nc.vector.tensor_tensor(x_all[:, k, :], ps_o, x_all[:, k, :], ALU.add).then_inc(x1_done, 1)

            def stats_2(k):
                dve.wait_ge(x1_done, k + 1)
                return mark(nc.vector.bn_stats(stats2[:, k % 2, :], x_all[:, k, :]))

            def norm_2(k):
                j = k % 2
                dve.wait_ge(rstd2_done, k + 1)
                if k == FIRST_RAW:
                    dve.wait_ge(sw_low, DC + 1)
                nc.vector.tensor_scalar(z_all[:, k, 0:D], x_all[:, k, :], mv2[:, j, 0:1], rstd2[:, j, :],
                                        ALU.subtract, ALU.mult).then_inc(z_done, 1)

            def z_low(k):
                dve.wait_ge(zh_done, k + 1)
                nc.vector.tensor_tensor(zTl[:, :, k * P:(k + 1) * P], zT.rearrange("p (c t) -> p c t", c=DC),
                                        zTh[:, :, k * P:(k + 1) * P].bitcast(F32), ALU.subtract).then_inc(zl_done, 1)

            def route(r):
                t = slice(r * RB, (r + 1) * RB)
                dve.wait_ge(el_done, (r + 1) * RB)
                link(nc.vector.tensor_scalar(sg[:, t, :], el[:, t, :], 1.0, None, ALU.add))
                link(nc.vector.reciprocal(sg[:, t, :], sg[:, t, :]))
                link(nc.vector.tensor_tensor(sbias[:, t, :], sg[:, t, :],
                                             bias[:, :].unsqueeze(1).broadcast_to([P, RB, E]), ALU.add))
                for i in range(r * RB, (r + 1) * RB):
                    last = nc.vector.max(top[:, i, :], sbias[:, i, :])
                link(last)
                for i in range(r * RB, (r + 1) * RB):
                    last = nc.vector.max_index(tidx[:, i, :], top[:, i, :], sbias[:, i, :])
                link(last)
                link(nc.vector.tensor_copy(fidx[:, t, :], tidx[:, t, 0:K]))
                for k in range(K):
                    last = nc.vector.tensor_tensor(pick[:, k, t, :], iota_e[:, :].unsqueeze(1).broadcast_to([P, RB, E]),
                                                   fidx[:, t, k:k + 1].broadcast_to([P, RB, E]), ALU.is_equal)
                link(last)
                nc.vector.tensor_tensor(both[:, t, :], pick[:, 0, t, :], pick[:, 1, t, :],
                                        ALU.add).then_inc(both_done, 1)

            def destinations():
                dve.wait_ge(rank_done, 1)
                count = rank[:, NT * E:(NT + 1) * E]
                link(nc.vector.tensor_copy(small[:, 0, :], count))
                link(nc.vector.tensor_tensor(big[:, :, :], small[:, 0, :].unsqueeze(2).broadcast_to([P, E, NT]),
                                             iota_n[:, :].unsqueeze(1).broadcast_to([P, E, NT]), ALU.is_gt))
                link(nc.vector.tensor_reduce(small[:, 1, :], big[:, :, :], AX.X, ALU.add))
                link(nc.vector.tensor_tensor(tri[:, :, :], lower[:, :, :],
                                             small[:, 1, :].unsqueeze(1).broadcast_to([P, E, E]), ALU.mult))
                link(nc.vector.tensor_reduce(small[:, 2, :], tri[:, :, :], AX.X, ALU.add))
                nc.vector.tensor_tensor(small[:, 3, :], small[:, 1, :], small[:, 2, :], ALU.add)
                link(nc.vector.scalar_tensor_tensor(sbias[:, :, :], small[:, 2, :].unsqueeze(1).broadcast_to([P, NT, E]),
                                                    float(P), rank[:, 0:NT * E].rearrange("p (t e) -> p t e", e=E),
                                                    ALU.mult, ALU.add))
                for k in range(K):
                    last = nc.vector.tensor_tensor([top, el][k][:, :, :], pick[:, k, :, :], sbias[:, :, :], ALU.mult)
                link(last)
                for k in range(K):
                    last = nc.vector.tensor_reduce(dest[:, k, :], [top, el][k][:, :, :], AX.X, ALU.add)
                link(last)
                nc.vector.tensor_copy(desti[:, :, :], dest[:, :, :]).then_inc(dest_done, 1)
                dve.wait_ge(z_done, NT)
                nc.vector.tensor_copy(z_all[:, :, D + 1], dest[:, 1, :]).then_inc(dest_done, 1)

            def table_and_weights():
                link(nc.vector.tensor_tensor(cmp_t[:, :, :], tileno[:, :].unsqueeze(2).broadcast_to([1, SLOTS, E]),
                                             small[0:1, 3, :].unsqueeze(1).broadcast_to([1, SLOTS, E]), ALU.is_ge))
                link(nc.vector.tensor_reduce(tab_f[:, :], cmp_t[:, :, :], AX.X, ALU.add))
                nc.vector.tensor_scalar(tab[:, :], tab_f[:, :], float(E - 1), None, ALU.min).then_inc(tab_done, 1)
                for k in range(K):
                    last = nc.vector.tensor_tensor([top, el][k][:, :, :], pick[:, k, :, :], sg[:, :, :], ALU.mult)
                link(last)
                for k in range(K):
                    last = nc.vector.tensor_reduce(wk[:, k, :], [top, el][k][:, :, :], AX.X, ALU.add)
                link(last)
                link(nc.vector.tensor_tensor(wsum[:, 0, :], wk[:, 0, :], wk[:, 1, :], ALU.add))
                link(nc.vector.reciprocal(wsum[:, 1, :], wsum[:, 0, :]))
                for k in range(K):
                    last = nc.vector.tensor_tensor(wk[:, k, :], wk[:, k, :], wsum[:, 1, :], ALU.mult)
                link(last)

            def shared_piece(n):
                if n < NG * SC:
                    m = CHUNK[n % SC]
                    dve.wait_ge(ssg_done, n + 1)
                    if n >= 2:
                        dve.wait_ge(shl_done, n - 1)
                    nc.vector.tensor_tensor(s_hm[0:m, n % 2, :], s_sg[0:m, n % 2, :], s_gu[n % 3][0:m, GN:2 * GN],
                                            ALU.mult).then_inc(shm_done, 1)
                if 0 <= n - 1 < NG * SC:
                    g, c = (n - 1) // SC, (n - 1) % SC
                    m = CHUNK[c]
                    dve.wait_ge(shh_done, n)
                    nc.vector.tensor_tensor(s_hl[0:m, g % 2, c, :], s_hm[0:m, (n - 1) % 2, :],
                                            s_hh[0:m, g % 2, c, :].bitcast(F32), ALU.subtract).then_inc(shl_done, 1)
                g, i = divmod(n - 1 - SC - 1, SC)
                if n - 1 - SC - 1 >= 0 and i < GT and g < NG:
                    shared_add(GT * g + i)

            def shared_add(t):
                dve.wait_ge(sdn_done, t + 1)
                nc.vector.tensor_tensor(x_all[:, t, :], s_dn[t % 2], x_all[:, t, :], ALU.add).then_inc(sacc_done, 1)

            def expert_low(n):
                dve.wait_ge(ew_high, n + 1)
                nc.vector.tensor_tensor(pieces[n][1], stage(n), pieces[n][0].bitcast(F32),
                                        ALU.subtract).then_inc(ew_low, 1)

            for p in STEPS:
                if live(p + 1):
                    norm_1(p + 1)
                if live(p - 1):
                    n_sum = inverse_sums(p - 1)
                if live(p - 2):
                    add_attention(p - 2)
                if live(p - 1):
                    values(p - 1, n_sum)
                if live(p - 2):
                    n_st2 = stats_2(p - 2)
                    n_st2 = aggregate(mv2[:, p % 2, :], stats2[:, p % 2, :], n_st2)
                if live(p - 3):
                    z_low(p - 3)
                if live(p - 2):
                    plus_eps(mv2[:, p % 2, :], n_st2, var2_done, 1.0)
                if live(p):
                    maxima(p, 0)
                if live(p + 2):
                    n_st1 = stats_1(p + 2)
                if live(p):
                    maxima(p, 1)
                if live(p + 2):
                    n_st1 = aggregate(mv[:, p % 2, :], stats[:, p % 2, :], n_st1)
                if live(p - 2):
                    norm_2(p - 2)
                if live(p + 2):
                    plus_eps(mv[:, p % 2, :], n_st1, var_done, SCALE)
                if p == 1:
                    dve.wait_ge(const_done, 7)
                if live(p - 4) and (p - 4) % RB == RB - 1 and p < NT + 3:
                    route((p - 4) // RB)
                if p == NT + 2:
                    route(NT // RB - 1)
                    destinations()
            for n in EARLY:
                shared_piece(n)
                if n == SC:
                    table_and_weights()
                if n < NP:
                    expert_low(n)
            dve.wait_ge(sc_done, B2 * NT)
            nc.vector.memset(hm[:, :, H:D], 0.0).then_inc(hm_pad, 1)

            for s in ESTEPS:
                if slot(s):
                    dve.wait_ge(exh_done, s + 1)
                    nc.vector.tensor_tensor(xl[:, s % 2, :], e_xt[s % 2], xh[:, s % 2, :].bitcast(F32),
                                            ALU.subtract).then_inc(exl_done, 1)
                    dve.wait_ge(xs_in[s % 3], 16 * (s // 3 + 1))
                    nc.vector.scalar_tensor_tensor(yi[:, s:s + 1], xs[s % 3][:, D + 1:D + 2], slotno[:, s:s + 1],
                                                   xs[s % 3][:, D:D + 1], ALU.is_equal, ALU.add).then_inc(yi_done, 1)
                if slot(s - 1):
                    t = s - 1
                    dve.wait_ge(esg_done, t + 1)
                    if t >= 2:
                        dve.wait_ge(eht_done, t - 1)
                    nc.vector.tensor_tensor(hm[:, t % 2, 0:H], esg[t % 2], e_gu[t % 2][:, H:2 * H],
                                            ALU.mult).then_inc(ehm_done, 1)
                if slot(s - 2):
                    t = s - 2
                    dve.wait_ge(ehh_done, t + 1)
                    nc.vector.tensor_tensor(hl[:, t % 2, :], e_ht[t % 2], hh[:, t % 2, :].bitcast(F32),
                                            ALU.subtract).then_inc(ehl_done, 1)

            def add_first(t):
                dve.wait_ge(yk_in[t % 4], 16 * (t // 4 + 1))
                dve.wait_ge(sacc_done, t + 1)
                nc.vector.scalar_tensor_tensor(x_all[:, t, :], att_flat[:, (t % 4) * K * D:((t % 4) * K + 1) * D],
                                               wk[:, 0, t:t + 1], x_all[:, t, :], ALU.mult, ALU.add).then_inc(y0_done, 1)

            for n in LATE:
                shared_piece(n)
                for t in tails_after(n):
                    add_first(t)
            shared_add(NT - 1)
            for t in range(tails_after(LATE[-1]).stop, NT):
                add_first(t)

        @block.tensor
        def _(pe):
            mm = nc.tensor.matmul

            def three(o, parts):
                for n, (ah, al, bh, bl) in enumerate(parts):
                    mm(o, ah, bh, start=(n == 0), stop=False)
                    mm(o, ah, bl, start=False, stop=False)
                    last = mm(o, al, bh, start=False, stop=(n == len(parts) - 1))
                return last

            def scores(k):
                j = k % 2
                pe.wait_ge(kq_low, k + 1)
                if k >= 2:
                    pe.wait_ge(exp_done, B2 * (k - 1))
                for b in range(B2):
                    r = slice(b * S, (b + 1) * S)
                    for c in range(DC):
                        e = slice(c * P, (c + 1) * P)
                        last = three(ps_s[j][b][:, c * D:(c + 1) * D],
                                     [(kh[r, j, e], kl[r, j, e], qh[r, j, :], ql[r, j, :])])
                    last.then_inc(sc_done, 1)

            def context_T(k):
                if k >= 1:
                    pe.wait_ge(vt_done, k)
                pe.wait_ge(c_in[k % NL], 16 * (k // NL + 1))
                for c in range(DC):
                    last = nc.tensor.transpose(ps_c[:, c * P:(c + 1) * P], cr[:, k % NL, c * P:(c + 1) * P], ident[:])
                last.then_inc(ct_done, 1)

            def attend(k):
                j = k % 2
                pe.wait_ge(vt_done, k + 1)
                if k >= 1:
                    pe.wait_ge(x1_done, k)
                for b in range(B2):
                    for c in range(DC):
                        m = (b * DC + c) * D
                        last = mm(ps_o[b * S:(b + 1) * S, :], vT[:, j, c, b, :], att[:, j, m:m + D],
                                  start=(c == 0), stop=(c == DC - 1))
                last.then_inc(out_done, 1)

            def z_T(k):
                pe.wait_ge(z_done, k + 1)
                if k >= 1:
                    pe.wait_ge(el_done, k)
                for c in range(DC):
                    last = nc.tensor.transpose(zT[:, c * P:(c + 1) * P], z_all[:, k, c * P:(c + 1) * P], ident[:])
                last.then_inc(zt_done, 1)

            def route_logits(k):
                pe.wait_ge(zl_done, k + 1)
                if k == 0:
                    pe.wait_ge(gw_done, 1)
                t = slice(k * P, (k + 1) * P)
                three(logits, [(zTh[:, c, t], zTl[:, c, t], gwh[:, c * E:(c + 1) * E], gwl[:, c * E:(c + 1) * E])
                               for c in range(DC)]).then_inc(lg_done, 1)

            def ranks(r):
                pe.wait_ge(both_done, r + 1)
                for t in range(r * RB, (r + 1) * RB):
                    mm(rank[:, t * E:(t + 1) * E], below[:], both[:, t, :], start=(t == 0), stop=False,
                       skip_group_check=True)
                    n = NT - t
                    last = mm(rank[:, (t + 1) * E:(NT + 1) * E], ones[:],
                              both[:, t:t + 1, :].broadcast_to([P, n, E]), start=False, stop=(t == NT - 1),
                              skip_group_check=True)
                if r == NT // RB - 1:
                    last.then_inc(rank_done, 1)

            def shared_up(g, c):
                n, m = SC * g + c, CHUNK[c]
                if n == 0:
                    pe.wait_ge(sw_low, DC + 1)
                    pe.wait_ge(exp_done, B2 * NT)
                if n >= 3:
                    pe.wait_ge(shm_done, n - 2)
                if c == 0:
                    pe.wait_ge(zl_done, GT * (g + 1))
                t = slice(g * GN, (g + 1) * GN)
                for h in range(2):
                    f = slice(h * HS + c * P, h * HS + c * P + m)
                    last = three(s_gu[n % 3][0:m, h * GN:(h + 1) * GN],
                                 [(suh[:, d, f], sul[:, d, f], zTh[:, d, t], zTl[:, d, t]) for d in range(DC)])
                last.then_inc(sup_done, 1)

            def shared_down(g, i):
                t = GT * g + i
                pe.wait_ge(shl_done, SC * (g + 1))
                if t >= 2:
                    pe.wait_ge(sacc_done, t - 1)
                if t == 1:
                    pe.wait_ge(vt_done, NT)
                s = slice(i * P, (i + 1) * P)
                three(s_dn[t % 2], [(s_hh[0:m, g % 2, c, s], s_hl[0:m, g % 2, c, s], sdh[0:m, c, :], sdl[0:m, c, :])
                                    for c, m in enumerate(CHUNK)]).then_inc(sdn_done, 1)

            def shared_piece(n):
                if n < NG * SC:
                    shared_up(n // SC, n % SC)
                g, i = divmod(n - SC - 1, SC)
                if n - SC - 1 >= 0 and i < GT and g < NG:
                    shared_down(g, i)

            def keep_warm(n, first=False):
                for i in range(n):
                    mm(bank[7][:, D:D + P], ident[:], ident[:], start=first and i == 0, stop=False, skip_group_check=True)

            pe.wait_ge(id_done, 1)
            keep_warm(WARM, first=True)
            for p in STEPS:
                if live(p):
                    scores(p)
                if live(p - 3):
                    route_logits(p - 3)
                if live(p):
                    context_T(p)
                if live(p - 1):
                    attend(p - 1)
                if live(p - 2):
                    z_T(p - 2)
                if live(p):
                    keep_warm(FILL)
                if p == 3:
                    pe.wait_ge(const_done, 7)
                if live(p - 4) and (p - 4) % RB == RB - 1 and p < NT + 3:
                    ranks((p - 4) // RB)
                if p == NT + 2:
                    ranks(NT // RB - 1)
                if p in AHEAD:
                    shared_piece(p - NT)
            for n in range(len(AHEAD), PAUSE):
                shared_piece(n)

            pe.wait_ge(tab_done, 1)
            pe.wait_ge(ew_low, NP)
            pe.wait_ge(hm_pad, 1)
            expert = {}
            for s in ESTEPS:
                if slot(s):
                    pe.wait_ge(xs_in[s % 3], 16 * (s // 3 + 1))
                    for c in range(DC):
                        last = nc.tensor.transpose(e_xt[s % 2][:, c * P:(c + 1) * P], xs[s % 3][:, c * P:(c + 1) * P],
                                                   ident[:])
                    last.then_inc(ext_done, 1)
                if slot(s - 1):
                    t, j = s - 1, (s - 1) % 2
                    expert[t] = pe.value_load(tab[0:1, t:t + 1], min_val=0, max_val=E - 1)
                    pe.wait_ge(exl_done, t + 1)
                    o = e_gu[j][:, 0:2 * H]
                    w = [[b[:, bass.ds(expert[t], 1), c * 2 * H:(c + 1) * 2 * H].rearrange("p a f -> p (a f)")
                          for b in (uph, upl)] for c in range(DC)]
                    three(o, [(xh[:, j, c * P:(c + 1) * P], xl[:, j, c * P:(c + 1) * P], w[c][0], w[c][1])
                              for c in range(DC)]).then_inc(eup_done, 1)
                if slot(s - 2):
                    t = s - 2
                    pe.wait_ge(ehm_done, t + 1)
                    for c in range(DC):
                        last = nc.tensor.transpose(e_ht[t % 2][:, c * P:(c + 1) * P], hm[:, t % 2, c * P:(c + 1) * P],
                                                   ident[:])
                    last.then_inc(eht_done, 1)
                if slot(s - 3):
                    t, j = s - 3, (s - 3) % 2
                    pe.wait_ge(ehl_done, t + 1)
                    w = [[b[:, bass.ds(expert[t], 1), c * D:(c + 1) * D].rearrange("p a f -> p (a f)")
                          for b in (dnh, dnl)] for c in range(DC)]
                    three(e_y[j], [(hh[:, j, c * P:(c + 1) * P], hl[:, j, c * P:(c + 1) * P], w[c][0], w[c][1])
                                   for c in range(DC)]).then_inc(edn_done, 1)

            pe.wait_ge(ey_done, SLOTS)
            for n in LATE:
                shared_piece(n)


def kernel(x, ctx_2048, L0_ffn_gate_w, L0_ffn_gate_bias, L0_ffn_shared_gw, L0_ffn_shared_dw, L0_ffn_up_w,
           L0_ffn_down_w):
    import numpy as np
    import concourse.bacc as bacc
    from concourse.bass_utils import run_bass_kernel_spmd

    x, ctx_kv = np.asarray(x), np.asarray(ctx_2048)
    up_w, down_w = np.asarray(L0_ffn_up_w), np.asarray(L0_ffn_down_w)
    sgw, sdw = np.asarray(L0_ffn_shared_gw), np.asarray(L0_ffn_shared_dw)
    P = 128
    E, D, H = down_w.shape
    HS = sdw.shape[1]
    DC, SC = D // P, -(-HS // P)
    up_wT = np.ascontiguousarray(up_w.transpose(2, 0, 1).reshape(DC, P, E, 2 * H).transpose(1, 2, 0, 3))
    down_wT = np.zeros((P, E, DC, D), x.dtype)
    for c in range(DC):
        h = down_w[:, :, c * P:min(H, (c + 1) * P)]
        down_wT[0:h.shape[2], :, c, :] = h.transpose(2, 0, 1)
    su = np.concatenate([sgw[HS:], sgw[:HS]]).T
    shared_upT = np.ascontiguousarray(su.reshape(DC, P, 2 * HS).transpose(1, 0, 2))
    shared_dnT = np.zeros((P, SC, D), x.dtype)
    for c in range(SC):
        h = sdw[:, c * P:min(HS, (c + 1) * P)]
        shared_dnT[0:h.shape[1], c, :] = h.T
    gate = np.ascontiguousarray(np.asarray(L0_ffn_gate_w).T.reshape(DC, P, E).transpose(1, 0, 2)).reshape(P, DC * E)
    gbias = np.ascontiguousarray(np.broadcast_to(np.asarray(L0_ffn_gate_bias), (P, E)))
    arrays = {"x": x.reshape(-1, D), "ctx_kv": ctx_kv.reshape(-1, D), "up_wT": up_wT.reshape(P, E, -1),
              "down_wT": down_wT.reshape(P, E, -1), "shared_upT": shared_upT, "shared_dnT": shared_dnT,
              "gate_wT": gate, "gate_bias": gbias}
    nc = bacc.Bacc("TRN2", target_bir_lowering=False, num_devices=1)
    aps = {n: nc.dram_tensor(n, a.shape, mybir.dt.from_np(a.dtype), kind="ExternalInput").ap()
           for n, a in arrays.items()}
    out = nc.dram_tensor("out", arrays["x"].shape, mybir.dt.float32, kind="ExternalOutput").ap()
    xattn_moe_kernel(nc, *aps.values(), out)
    r = run_bass_kernel_spmd(nc, [{n: np.ascontiguousarray(a) for n, a in arrays.items()}], core_ids=[0])
    return r.results[0]["out"].reshape(x.shape)
```
